# Optimizing a Trainium2 kernel written in Bass

```python
import numpy as np
import jax
import jax.numpy as jnp

def _softmax(x, axis=-1):
    return jax.nn.softmax(x, axis=axis)

def _gelu(x):
    return jax.nn.gelu(x, approximate=True)

def _silu(x):
    return jax.nn.silu(x)

def _sigmoid(x):
    return jax.nn.sigmoid(x)

def _layernorm(x, axis=-1, eps=1e-05):
    m = jnp.mean(x, axis=axis, keepdims=True)
    v = jnp.var(x, axis=axis, keepdims=True)
    return (x - m) / jnp.sqrt(v + eps)

def _scatter_add(tgt, idx, src, axis=0):
    return tgt.at[idx].add(src)

def _segment_sum(src, seg, n):
    return jax.ops.segment_sum(src, seg, n)
kernel_name = 'mk_gnn_resnorm_d1_gnn_r8_827ac8'

def setup_inputs(seed: int=0):
    np.random.seed(seed)
    _w = jnp.asarray

    def _rec_inputs():
        import jax
        import jax.numpy as jnp
        _gk = jax.random.key(seed)
        x = -0.000202 + 1 * jax.random.normal(jax.random.fold_in(_gk, 1), (12500, 64), jnp.float32)
        src = jax.random.randint(jax.random.fold_in(_gk, 2), (200000,), 0, 12500, jnp.int32)
        dst = jnp.minimum((12500 * jax.random.uniform(jax.random.fold_in(_gk, 3), (200000,)) ** 2.0).astype(jnp.int32), 99999)
        _o = jnp.argsort(dst, stable=True)
        src = src[_o]
        dst = dst[_o]
        edge_attr_41 = -0.000138925 + 0.999911 * jax.random.normal(jax.random.fold_in(_gk, 12), (200000, 41), jnp.float32)
        return (x, src, dst, edge_attr_41)
    x, src, dst, edge_attr_41 = _rec_inputs()

    def _L0_gnn_setup():
        import jax, jax.numpy as jnp
        import numpy as np
        N_NODES = 12500
        N_EDGES = 150000
        NODE_F = 64
        EDGE_F = 41
        EPS = 1e-05

        def _bn(x, gamma, beta):
            m = x.mean(axis=0)
            v = x.var(axis=0)
            return gamma * (x - m) * jax.lax.rsqrt(v + EPS) + beta
        key = jax.random.key(seed)
        ks = jax.random.split(key, 12)
        cat = 2 * NODE_F + EDGE_F
        return {'node_feats': jax.random.normal(ks[0], (N_NODES, NODE_F), dtype=jnp.float32), 'edge_feats': jax.random.normal(ks[1], (N_EDGES, EDGE_F), dtype=jnp.float32), 'src': jax.random.randint(ks[2], (N_EDGES,), 0, N_NODES, dtype=jnp.int32), 'dst': jax.random.randint(ks[3], (N_EDGES,), 0, N_NODES, dtype=jnp.int32), 'W1': jax.random.normal(ks[4], (NODE_F, cat), dtype=jnp.float32) / np.sqrt(cat), 'b1': jnp.zeros((NODE_F,), dtype=jnp.float32), 'W2': jax.random.normal(ks[5], (NODE_F, cat), dtype=jnp.float32) / np.sqrt(cat), 'b2': jnp.zeros((NODE_F,), dtype=jnp.float32), 'g1': jnp.ones((NODE_F,), dtype=jnp.float32), 'bt1': jnp.zeros((NODE_F,), dtype=jnp.float32), 'g2': jnp.ones((NODE_F,), dtype=jnp.float32), 'bt2': jnp.zeros((NODE_F,), dtype=jnp.float32), 'g3': jnp.ones((NODE_F,), dtype=jnp.float32), 'bt3': jnp.zeros((NODE_F,), dtype=jnp.float32)}
    _L0_gnn_all = _L0_gnn_setup()
    _L0_gnn_in = {k: v for k, v in _L0_gnn_all.items() if k in ('W1', 'b1', 'W2', 'b2', 'g1', 'bt1', 'g2', 'bt2', 'g3', 'bt3')}
    del _L0_gnn_all
    return {'x': x, 'src': src, 'dst': dst, 'edge_attr_41': edge_attr_41, 'L0_gnn_W1': _L0_gnn_in['W1'], 'L0_gnn_b1': _L0_gnn_in['b1'], 'L0_gnn_W2': _L0_gnn_in['W2'], 'L0_gnn_b2': _L0_gnn_in['b2'], 'L0_gnn_g1': _L0_gnn_in['g1'], 'L0_gnn_bt1': _L0_gnn_in['bt1'], 'L0_gnn_g2': _L0_gnn_in['g2'], 'L0_gnn_bt2': _L0_gnn_in['bt2'], 'L0_gnn_g3': _L0_gnn_in['g3'], 'L0_gnn_bt3': _L0_gnn_in['bt3']}

def reference(x, src, dst, edge_attr_41, L0_gnn_W1, L0_gnn_b1, L0_gnn_W2, L0_gnn_b2, L0_gnn_g1, L0_gnn_bt1, L0_gnn_g2, L0_gnn_bt2, L0_gnn_g3, L0_gnn_bt3):
    import jax
    import jax.numpy as jnp

    def _L0_gnn_ref(node_feats, edge_feats, src, dst, W1, b1, W2, b2, g1, bt1, g2, bt2, g3, bt3):
        import jax, jax.numpy as jnp
        import numpy as np
        N_NODES = 12500
        N_EDGES = 150000
        NODE_F = 64
        EDGE_F = 41
        EPS = 1e-05

        def _bn(x, gamma, beta):
            m = x.mean(axis=0)
            v = x.var(axis=0)
            return gamma * (x - m) * jax.lax.rsqrt(v + EPS) + beta
        total_edge = jnp.concatenate([node_feats[src], node_feats[dst], edge_feats], axis=-1)
        nbr_filter = jax.nn.sigmoid(_bn(total_edge @ W1.T + b1, g1, bt1))
        nbr_core = jax.nn.softplus(_bn(nbr_filter, g2, bt2))
        h = nbr_filter * nbr_core
        agg = jax.ops.segment_sum(h, dst, num_segments=N_NODES)
        new_node = _bn(agg, g3, bt3)
        return node_feats + new_node
    x = _layernorm(x + _L0_gnn_ref(x, edge_attr_41, src, dst, L0_gnn_W1, L0_gnn_b1, L0_gnn_W2, L0_gnn_b2, L0_gnn_g1, L0_gnn_bt1, L0_gnn_g2, L0_gnn_bt2, L0_gnn_g3, L0_gnn_bt3), axis=-1)
    return x

_drawn_inputs = setup_inputs


def setup_inputs(seed=0):
    import zlib

    import numpy as np

    out = dict(_drawn_inputs(seed))
    spreads = {'L0_gnn_b1': (0.0, 2.0),
     'L0_gnn_b2': (0.0, 0.1),
     'L0_gnn_g1': (1.0, 0.6),
     'L0_gnn_bt1': (0.0, 0.8),
     'L0_gnn_g2': (1.0, 0.6),
     'L0_gnn_bt2': (0.0, 2.0),
     'L0_gnn_g3': (1.0, 0.2),
     'L0_gnn_bt3': (0.0, 0.1)}
    factors = {}
    for name, (base, spread) in spreads.items():
        noise = np.random.default_rng([zlib.crc32(name.encode()), seed]).standard_normal(out[name].shape)
        drawn = base * np.exp(spread * noise) if base else spread * noise
        out[name] = jnp.asarray(drawn.astype(out[name].dtype))
    for name, factor in factors.items():
        out[name] = (out[name] * factor).astype(out[name].dtype)
    return out
```

```python
import numpy as np
import concourse.bass as bass
from concourse import mybir
from contextlib import ExitStack

F32 = mybir.dt.float32
I32 = mybir.dt.int32
ALU = mybir.AluOpType
ACT = mybir.ActivationFunctionType
AX = mybir.AxisListType

N_NODES, N_EDGES, F, EDGE_F = 12500, 200000, 64, 41
EPS = 1e-5

P = 128
HALF = 512
TILES = HALF // P
GROUPS = N_EDGES // (2 * HALF)
CHUNK = 3
CHUNKS = GROUPS // CHUNK
WIDE = CHUNK * HALF
T_HALF = (N_EDGES - GROUPS * 2 * HALF) // 2
T_P = 80
T_TILES = T_HALF // T_P
HALVES = 2 * GROUPS + 2
MAIN = GROUPS * 2 * HALF

WIN = 128
WINDOWS = -(-N_NODES // WIN)
N_PAD = WINDOWS * WIN
BLOCK = 7
BLOCKS = WINDOWS // BLOCK

E_ROWS = 48
D_ROWS, D_HALVES = 78, 5
EXP_CAP = 1e18


class Halves:

    def __init__(self, half, tile):
        self.half, self.tile, self.tiles = half, tile, half // tile


FULL, RAGGED = Halves(HALF, P), Halves(T_HALF, T_P)


def after(eng, sem, count):
    if isinstance(count, int) and count <= 0:
        return
    eng.wait_ge(sem, count)


def rounds(eng, total, slots, body):
    for s in range(slots):
        body(s, s, 0)
    turns = total // slots
    with eng.Fori(1, turns) as i:
        for s in range(slots):
            body(i * slots + s, s, i)
    for s in range(total - turns * slots):
        body(turns * slots + s, s, turns)


def build(nc, xt, x_nodes, src_t, src_r, dst_t, dst_r, dst_h, dst_hr, e_main, e_ragged,
          w_nodes, w_edges, b1, g1, bt1, g2, bt2, g3, bt3, out):
    ctx = ExitStack()
    with ctx:
        def dram(name, shape, dt=F32):
            return nc.dram_tensor(name, shape, dt, kind="Internal").ap()

        p_table = dram("p_table", [N_PAD, F])
        q_table = dram("q_table", [N_PAD, F])
        dst_f = dram("dst_f", [1, N_EDGES])
        base_f = dram("base_f", [1, HALVES])
        base_i = dram("base_i", [1, HALVES], I32)
        reach = dram("reach", [1, HALVES])
        edge_mem = dram("edge_mem", [CHUNKS, P, CHUNK, HALF])
        edge_mem_r = dram("edge_mem_r", [P, T_HALF])

        held = ExitStack()
        ctx.enter_context(held)

        def keep(name, shape, dt=F32):
            return held.enter_context(nc.sbuf_tensor(name, shape, dt))

        def sem(name):
            return ctx.enter_context(nc.semaphore(name))

        ident = keep("ident", [P, P])
        fold = keep("fold", [P, P])
        base_s = keep("base_s", [1, HALVES], I32)
        flag = keep("flag", [1, 1], I32)
        fits = keep("fits", [1, 4])
        node_col = keep("node_col", [P, HALVES])
        win_col = keep("win_col", [P, WINDOWS])
        rel = keep("rel", [P, GROUPS, 2, TILES])
        rel_r = keep("rel_r", [T_P, 2, T_TILES])
        dst_tf = keep("dst_tf", [P, GROUPS, 2, TILES])
        dst_rf = keep("dst_rf", [T_P, 2, T_TILES])
        iota_row = keep("iota_row", [P, WIN])
        win_start = keep("win_start", [P, WINDOWS])
        src_idx = keep("src_idx", [P, GROUPS, 2 * TILES], I32)
        src_idx_r = keep("src_idx_r", [T_P, 2 * T_TILES], I32)
        w_edge = keep("w_edge", [2 * E_ROWS, P])
        ones = keep("ones", [1, P])
        gb = keep("gb", [P, 6])
        bn1 = keep("bn1", [P, 2])
        bn2 = keep("bn2", [P, 2])
        bn3 = keep("bn3", [P, 2])
        tmp = keep("tmp", [P, 12])
        pair_ps = held.enter_context(nc.psum_tensor("pair_ps", [P, 512], F32))

        stage = ExitStack()
        with stage:
            def sb(name, shape, dt=F32):
                return stage.enter_context(nc.sbuf_tensor(name, shape, dt))

            x_in = [sb(f"x_in{s}", [F, BLOCK, P]) for s in range(2)]
            w_node = sb("w_node", [F, 2 * F])
            b1_all = sb("b1_all", [P, F])
            p_out = [sb(f"p_out{s}", [P, BLOCK, F]) for s in range(2)]
            q_out = [sb(f"q_out{s}", [P, BLOCK, F]) for s in range(2)]
            dst_hi = sb("dst_hi", [D_ROWS, D_HALVES, HALF], I32)
            dst_hf = sb("dst_hf", [D_ROWS, D_HALVES, HALF])
            dst_ri = sb("dst_ri", [2, T_HALF], I32)
            dst_rrf = sb("dst_rrf", [2, T_HALF])
            low = sb("low", [D_ROWS, 3, D_HALVES])
            low_r = sb("low_r", [2, 3, 1])
            low_i = sb("low_i", [D_ROWS, D_HALVES], I32)
            low_ri = sb("low_ri", [2, 1], I32)
            base_all = sb("base_all", [P, HALVES])
            reach_row = sb("reach_row", [1, HALVES])
            dst_ti = sb("dst_ti", [P, GROUPS, 2, TILES], I32)
            dst_tri = sb("dst_tri", [T_P, 2, T_TILES], I32)
            iota_p = sb("iota_p", [P, 1])
            nodes_ps = [stage.enter_context(nc.psum_tensor(f"nodes_ps{s}", [P, 8, P], F32)) for s in range(2)]

            w_in, dst_in, tiles_in = sem("w_in"), sem("dst_in"), sem("tiles_in")
            x_loaded = [sem(f"x_loaded{s}") for s in range(2)]
            projected, pq_copied, q_copied = sem("projected"), sem("pq_copied"), sem("q_copied")
            pq_stored = [sem(f"pq_stored{s}") for s in range(2)]
            dst_cast, lows, bases_out, bases_in = sem("dst_cast"), sem("lows"), sem("bases_out"), sem("bases_in")
            made, made_v, masks = sem("made"), sem("made_v"), sem("masks")
            ve = sem("ve")

            blk = stage.enter_context(nc.Block())

            @blk.sync
            def _(sp):
                sp.dma_start(dst_hi[:], dst_h).then_inc(dst_in, 16)
                sp.dma_start(dst_ri[:], dst_hr).then_inc(dst_in, 16)
                sp.dma_start(w_node[:], w_nodes).then_inc(w_in, 16)
                sp.dma_start(b1_all[:], b1.partition_broadcast(P)).then_inc(w_in, 16)
                sp.dma_start(w_edge[:], w_edges).then_inc(w_in, 16)
                for n, v in enumerate((g1, bt1, g2, bt2, g3, bt3)):
                    for h in range(2):
                        sp.dma_start(gb[h * F:(h + 1) * F, n:n + 1], v.rearrange("(f a) -> f a", a=1)).then_inc(w_in, 16)
                sp.dma_start(src_idx[:], src_t).then_inc(tiles_in, 16)
                sp.dma_start(src_idx_r[:], src_r).then_inc(tiles_in, 16)
                sp.dma_start(dst_ti[:], dst_t).then_inc(tiles_in, 16)
                sp.dma_start(dst_tri[:], dst_r).then_inc(tiles_in, 16)

                def load_x(n, s, turn):
                    after(sp, projected, n - 1)
                    sp.dma_start(x_in[s][:], xt[bass.ds(n, 1)].rearrange("a f b p -> (a f) b p")).then_inc(x_loaded[s], 16)
                rounds(sp, BLOCKS, 2, load_x)

            @blk.tensor
            def _(pe):
                def project(n, s, turn):
                    pe.wait_ge(x_loaded[s], 16 * turn + 16)
                    if isinstance(n, int) and n == 0:
                        pe.wait_ge(w_in, 15 * 16)
                    after(pe, pq_copied, n - 1)
                    after(pe, q_copied, n - 1)
                    for b in range(BLOCK):
                        mm = pe.matmul(nodes_ps[s][:, b, :], x_in[s][:, b, :], w_node[:], start=True, stop=True)
                    mm.then_inc(projected, 1)
                rounds(pe, BLOCKS, 2, project)

            @blk.scalar
            def _(act):
                q_view = q_table.rearrange("(p n b) f -> n p b f", p=P, b=BLOCK)
                p_view = p_table.rearrange("(p n b) f -> n p b f", p=P, b=BLOCK)

                def q_part(n, s, turn):
                    act.wait_ge(pq_copied, n + 1)
                    after(act, pq_stored[s], 32 * turn)
                    act.activation(q_out[s][:], nodes_ps[s][:, 0:BLOCK, F:2 * F], ACT.Copy).then_inc(q_copied, 1)
                    act.wait_ge(q_copied, n + 1)
                    act.dma_start(q_view[bass.ds(n, 1)].rearrange("a p b f -> (a p) b f"), q_out[s][:]).then_inc(pq_stored[s], 16)
                    act.dma_start(p_view[bass.ds(n, 1)].rearrange("a p b f -> (a p) b f"), p_out[s][:]).then_inc(pq_stored[s], 16)
                rounds(act, BLOCKS, 2, q_part)
                for s in range(2):
                    act.wait_ge(pq_stored[s], 32 * (BLOCKS // 2))

            @blk.gpsimd
            def _(gp):
                gp.iota(iota_row[:], [[1, WIN]], base=0, channel_multiplier=0, allow_small_or_imprecise_dtypes=True).then_inc(made, 1)
                gp.iota(iota_p[:], [[0, 1]], base=0, channel_multiplier=1, allow_small_or_imprecise_dtypes=True).then_inc(made, 1)
                gp.iota(win_col[:], [[WIN, WINDOWS]], base=0, channel_multiplier=1, allow_small_or_imprecise_dtypes=True).then_inc(made, 1)
                gp.iota(win_start[:], [[WIN, WINDOWS]], base=0, channel_multiplier=0, allow_small_or_imprecise_dtypes=True).then_inc(made, 1)
                for t in (ident, fold):
                    gp.memset(t[:], 0.0).then_inc(masks, 1)
                gp.memset(ones[:], 1.0).then_inc(made, 1)
                gp.wait_ge(masks, 2)
                gp.affine_select(out=ident[:], in_=ident[:], compare_op=ALU.not_equal, fill=1.0, base=0,
                                 pattern=[[-1, P]], channel_multiplier=1).then_inc(masks, 1)
                gp.affine_select(out=fold[:], in_=fold[:], compare_op=ALU.not_equal, fill=1.0, base=0,
                                 pattern=[[-1, P]], channel_multiplier=1).then_inc(masks, 1)
                gp.wait_ge(masks, 4)
                gp.affine_select(out=fold[:], in_=fold[:], compare_op=ALU.not_equal, fill=1.0, base=-F,
                                 pattern=[[-1, P]], channel_multiplier=1).then_inc(masks, 1)
                gp.wait_ge(masks, 5)
                gp.affine_select(out=fold[:], in_=fold[:], compare_op=ALU.not_equal, fill=1.0, base=F,
                                 pattern=[[-1, P]], channel_multiplier=1).then_inc(masks, 1)
                gp.wait_ge(masks, 6)

                gp.wait_ge(dst_cast, 2)
                gp.dma_start(dst_f[:, 0:MAIN].rearrange("a (p w) -> (a p) w", p=D_ROWS),
                             dst_hf[:].rearrange("p h w -> p (h w)")).then_inc(bases_out, 16)
                gp.dma_start(dst_f[:, MAIN:].rearrange("a (p w) -> (a p) w", p=2), dst_rrf[:]).then_inc(bases_out, 16)
                gp.wait_ge(lows, 2)
                for row, main, ragged in ((base_f, low[:, 0, :], low_r[:, 0, :]), (base_i, low_i[:], low_ri[:]),
                                          (reach, low[:, 2, :], low_r[:, 2, :])):
                    gp.dma_start(row[:, 0:2 * GROUPS].rearrange("a (p h) -> (a p) h", p=D_ROWS), main).then_inc(bases_out, 16)
                    gp.dma_start(row[:, 2 * GROUPS:].rearrange("a (p h) -> (a p) h", p=2), ragged).then_inc(bases_out, 16)
                gp.wait_ge(bases_out, 8 * 16)
                gp.dma_start(base_s[:], base_i).then_inc(bases_in, 16)
                gp.dma_start(reach_row[:], reach).then_inc(bases_in, 16)
                gp.dma_start(base_all[:], base_f.rearrange("a h -> (a h)").partition_broadcast(P)).then_inc(bases_in, 16)

            @blk.vector
            def _(v):
                v.wait_ge(dst_in, 32)
                v.tensor_copy(dst_hf[:], dst_hi[:]).then_inc(dst_cast, 1)
                v.tensor_copy(dst_rrf[:], dst_ri[:]).then_inc(dst_cast, 1)
                v.wait_ge(dst_cast, 2)
                for full, wide, lo, lo_i in ((True, dst_hf, low, low_i), (False, dst_rrf, low_r, low_ri)):
                    shown = wide[:] if full else wide[:].rearrange("p (a w) -> p a w", a=1)
                    v.tensor_reduce(lo[:, 0, :], shown, AX.X, ALU.min).then_inc(ve, 1)
                    v.tensor_reduce(lo[:, 1, :], shown, AX.X, ALU.max).then_inc(ve, 1)
                v.wait_ge(ve, 4)
                for lo in (low, low_r):
                    v.tensor_scalar(lo[:, 0, :], lo[:, 0, :], float(N_PAD - WIN), None, ALU.min).then_inc(ve, 1)
                v.wait_ge(ve, 6)
                for lo, lo_i in ((low, low_i), (low_r, low_ri)):
                    v.tensor_copy(lo_i[:], lo[:, 0, :]).then_inc(ve, 1)
                    v.tensor_tensor(lo[:, 2, :], lo[:, 1, :], lo[:, 0, :], ALU.subtract).then_inc(ve, 1)
                v.wait_ge(ve, 10)
                v.sem_inc(lows, 2)

                def p_part(n, s, turn):
                    v.wait_ge(projected, n + 1)
                    after(v, pq_stored[s], 32 * turn)
                    v.tensor_tensor(p_out[s][:], nodes_ps[s][:, 0:BLOCK, 0:F],
                                    b1_all[:].rearrange("p (a f) -> p a f", a=1).broadcast_to([P, BLOCK, F]), ALU.add).then_inc(pq_copied, 1)
                rounds(v, BLOCKS, 2, p_part)

                v.wait_ge(bases_in, 48)
                v.wait_ge(made, 5)
                v.wait_ge(tiles_in, 64)
                v.tensor_scalar(node_col[:], base_all[:], iota_p[:], None, ALU.add).then_inc(ve, 1)
                v.tensor_copy(dst_tf[:], dst_ti[:]).then_inc(ve, 1)
                v.tensor_copy(dst_rf[:], dst_tri[:]).then_inc(ve, 1)
                v.tensor_reduce(fits[:, 0:1], reach_row[:], AX.X, ALU.max).then_inc(ve, 1)
                v.wait_ge(ve, 14)
                v.tensor_scalar(fits[:, 1:2], fits[:, 0:1], float(WIN), None, ALU.is_ge).then_inc(ve, 1)
                main = base_all[:, 0:2 * GROUPS].rearrange("p (g h a) -> p g h a", h=2, a=1).broadcast_to([P, GROUPS, 2, TILES])
                v.tensor_tensor(rel[:], dst_tf[:], main, ALU.subtract).then_inc(ve, 1)
                last = base_all[0:T_P, 2 * GROUPS:].rearrange("p (h a) -> p h a", a=1).broadcast_to([T_P, 2, T_TILES])
                v.tensor_tensor(rel_r[:], dst_rf[:], last, ALU.subtract).then_inc(ve, 1)
                v.wait_ge(ve, 17)
                v.tensor_copy(flag[:], fits[:, 1:2]).then_inc(ve, 1)
                v.wait_ge(ve, 18)

        stage = ExitStack()
        with stage:
            def sb(name, shape, dt=F32):
                return stage.enter_context(nc.sbuf_tensor(name, shape, dt))

            S = 3
            rows = [sb(f"rows{s}", [P, TILES, 2, F]) for s in range(S)]
            e_in = [sb(f"e_in{s}", [2 * E_ROWS, HALF]) for s in range(S)]
            q_in = [sb(f"q_in{s}", [P, 2, F]) for s in range(S)]
            d_in = [sb(f"d_in{s}", [1, 2, HALF]) for s in range(S)]
            idx = [sb(f"idx{s}", [P, 2 * TILES], I32) for s in range(S)]
            z_sb = [sb(f"z_sb{s}", [P, HALF]) for s in range(S)]
            hot = sb("hot", [P, 2, HALF])
            qw_in = sb("qw_in", [P, F])
            stats = sb("stats", [P, GROUPS + 1, 6])
            z_ps = [stage.enter_context(nc.psum_tensor(f"z_ps{s}", [P, HALF], F32)) for s in range(S)]
            d_ps = stage.enter_context(nc.psum_tensor("d_ps", [P, 2, HALF], F32))

            loaded = [sem(f"loaded{s}") for s in range(S)]
            q_loaded = [sem(f"q_loaded{s}") for s in range(S)]
            gathered = [sem(f"gathered{s}") for s in range(S)]
            z_stored = [sem(f"z_stored{s}") for s in range(S)]
            idx_ready, dst_spread, hot_ready = sem("idx_ready"), sem("dst_spread"), sem("hot_ready")
            z_ready, z_copied, z_counted = sem("z_ready"), sem("z_copied"), sem("z_counted")
            gather_on, sweep_on = sem("gather_on"), sem("sweep_on")
            win_loaded, win_hot, win_used = sem("win_loaded"), sem("win_hot"), sem("win_used")
            aggr, paired, rooted, bn1_steps = sem("aggr"), sem("paired"), sem("rooted"), sem("bn1_steps")

            blk = stage.enter_context(nc.Block())

            def slot_of(g):
                return g % S

            @blk.sync
            def _(sp):
                def load(g, s, turn, size, general):
                    after(sp, z_ready, g - S + 1)
                    if size is FULL:
                        sp.dma_start(e_in[s][:], e_main[bass.ds(g, 1)].rearrange("a r w -> (a r) w")).then_inc(loaded[s], 16)
                    else:
                        sp.dma_start(e_in[s][:, 0:size.half], e_ragged).then_inc(loaded[s], 16)
                    sp.dma_start(d_in[s][:, :, 0:size.half],
                                 dst_f[:, bass.ds(g * 2 * HALF, 2 * size.half)].rearrange("a (h w) -> a h w", h=2)).then_inc(loaded[s], 16)
                    if not general:
                        for h in range(2):
                            base = sp.value_load(base_s[:, bass.ds(g * 2 + h, 1)], min_val=0, max_val=N_PAD - WIN)
                            sp.dma_start(q_in[s][:, h, :], q_table[bass.ds(base, WIN), :]).then_inc(q_loaded[s], 16)
                    else:
                        with sp.Fori(0, WINDOWS) as w:
                            sp.wait_ge(win_used, g * WINDOWS + w + 1)
                            sp.dma_start(qw_in[:], q_table[bass.ds(w * WIN, WIN), :]).then_inc(win_loaded, 16)

                def all_groups(general):
                    rounds(sp, GROUPS, S, lambda g, s, turn: load(g, s, turn, FULL, general))
                    load(GROUPS, slot_of(GROUPS), GROUPS // S, RAGGED, general)

                spread = sp.value_load(flag[:], min_val=0, max_val=1)
                with sp.If(spread < 1):
                    all_groups(False)
                with sp.Else():
                    all_groups(True)
                sp.nop()

            @blk.gpsimd
            def _(gp):
                def gather(g, s, turn, size):
                    gp.wait_ge(idx_ready, g + 1)
                    after(gp, z_ready, g - S + 1)
                    gp.sem_inc(gather_on, 1)
                    for t in range(size.tiles):
                        for h in range(2):
                            j = h * size.tiles + t
                            gp.indirect_dma_start(out=rows[s][0:size.tile, t, h, :], out_offset=None, in_=p_table,
                                                  in_offset=bass.IndirectOffsetOnAxis(ap=idx[s][0:size.tile, j:j + 1], axis=0)
                                                  ).then_inc(gathered[s], 16)
                rounds(gp, GROUPS, S, lambda g, s, turn: gather(g, s, turn, FULL))
                gather(GROUPS, slot_of(GROUPS), GROUPS // S, RAGGED)

            @blk.tensor
            def _(pe):
                def group(g, s, turn, size, general):
                    w = size.half
                    pe.wait_ge(loaded[s], 32 * turn + 32)
                    after(pe, hot_ready, g)
                    for h in range(2):
                        mm = pe.matmul(d_ps[:, h, 0:w], ones[:], d_in[s][:, h, 0:w], start=True, stop=True)
                    mm.then_inc(dst_spread, 1)
                    after(pe, z_copied, g - S + 1)
                    pe.matmul(z_ps[s][:, 0:w], w_edge[:], e_in[s][:, 0:w], start=True, stop=False)
                    pe.wait_ge(gathered[s], turn * 2 * TILES * 16 + 2 * size.tiles * 16)

                    def gathered_rows(last):
                        for t in range(size.tiles):
                            mm = pe.matmul(z_ps[s][:, t * size.tile:(t + 1) * size.tile],
                                           rows[s][0:size.tile, t, :, :].rearrange("p h f -> p (h f)"),
                                           ident[0:size.tile, 0:size.tile], start=False, stop=last)
                        return mm

                    def windows(which, last):
                        for h in range(2):
                            mm = pe.matmul(z_ps[s][h * F:(h + 1) * F, 0:w], which(h), hot[:, h, 0:w], start=False, stop=last)
                        return mm

                    if not general:
                        gathered_rows(False)
                        pe.wait_ge(q_loaded[s], 32 * turn + 32)
                        pe.wait_ge(hot_ready, g + 1)
                        windows(lambda h: q_in[s][:, h, :], True).then_inc(z_ready, 1)
                    else:
                        pe.sem_inc(sweep_on, 1)
                        with pe.Fori(0, WINDOWS) as k:
                            pe.wait_ge(win_loaded, (g * WINDOWS + k + 1) * 16)
                            pe.wait_ge(win_hot, g * WINDOWS + k + 1)
                            windows(lambda h: qw_in[:], False).then_inc(win_used, 1)
                        gathered_rows(True).then_inc(z_ready, 1)

                def all_groups(general):
                    rounds(pe, GROUPS, S, lambda g, s, turn: group(g, s, turn, FULL, general))
                    group(GROUPS, slot_of(GROUPS), GROUPS // S, RAGGED, general)

                spread = pe.value_load(flag[:], min_val=0, max_val=1)
                with pe.If(spread < 1):
                    all_groups(False)
                with pe.Else():
                    pe.sem_inc(win_used, 1)
                    all_groups(True)
                pe.wait_ge(aggr, 1)
                pe.matmul(pair_ps[:, 0:1], fold[:], tmp[:, 0:1], start=True, stop=True).then_inc(paired, 1)
                pe.wait_ge(aggr, 2)
                pe.matmul(pair_ps[:, 1:2], fold[:], tmp[:, 4:5], start=True, stop=True).then_inc(paired, 1)

            @blk.scalar
            def _(act):
                def copy(g, s, turn, size):
                    act.wait_ge(z_ready, g + 1)
                    after(act, z_counted, g - S + 1)
                    after(act, z_stored[s], 16 * turn)
                    act.activation(z_sb[s][:, 0:size.half], z_ps[s][:, 0:size.half], ACT.Copy).then_inc(z_copied, 1)
                    act.wait_ge(z_copied, g + 1)
                    if size is FULL:
                        to = edge_mem[bass.ds(turn, 1), :, s, :].rearrange("c p w -> (c p) w")
                    else:
                        to = edge_mem_r
                    act.dma_start(to, z_sb[s][:, 0:size.half]).then_inc(z_stored[s], 16)
                rounds(act, GROUPS, S, lambda g, s, turn: copy(g, s, turn, FULL))
                copy(GROUPS, slot_of(GROUPS), GROUPS // S, RAGGED)
                for s in range(S):
                    act.wait_ge(z_stored[s], 16 * (GROUPS // S + (s == slot_of(GROUPS))))
                act.wait_ge(aggr, 3)
                act.activation(tmp[:, 7:8], tmp[:, 6:7], ACT.Sqrt).then_inc(rooted, 1)

            @blk.vector
            def _(v):
                def indices(g, s, turn):
                    v.tensor_copy(idx[s][:], src_idx[:, bass.ds(g, 1), :].rearrange("p a j -> p (a j)")).then_inc(idx_ready, 1)

                def group(g, s, turn, size, general, more):
                    v.wait_ge(dst_spread, g + 1)
                    after(v, z_ready, g)
                    if not general:
                        for h in range(2):
                            hots = v.tensor_scalar(hot[:, h, 0:size.half], d_ps[:, h, 0:size.half],
                                                   node_col[:, bass.ds(g * 2 + h, 1)], None, ALU.is_equal)
                        hots.then_inc(hot_ready, 1)
                    else:
                        v.sem_inc(sweep_on, 1)
                        with v.Fori(0, WINDOWS) as k:
                            v.wait_ge(win_used, g * WINDOWS + k + 1)
                            for h in range(2):
                                hots = v.tensor_scalar(hot[:, h, 0:size.half], d_ps[:, h, 0:size.half],
                                                       win_col[:, bass.ds(k, 1)], None, ALU.is_equal)
                            hots.then_inc(win_hot, 1)
                        v.sem_inc(hot_ready, 1)
                    v.wait_ge(z_copied, g + 1)
                    v.bn_stats(stats[:, bass.ds(g, 1), :].rearrange("p a k -> p (a k)"), z_sb[s][:, 0:size.half]).then_inc(z_counted, 1)
                    if more:
                        indices(g + S, s, turn + 1)

                def all_groups(general):
                    for g in range(S):
                        group(g, g, 0, FULL, general, True)
                    with v.Fori(1, GROUPS // S - 1) as i:
                        for s in range(S):
                            group(i * S + s, s, i, FULL, general, True)
                    for s in range(S):
                        g = GROUPS - S + s
                        group(g, s, GROUPS // S - 1, FULL, general, False)
                        if s == slot_of(GROUPS):
                            v.tensor_copy(idx[s][0:T_P, 0:2 * T_TILES], src_idx_r[:]).then_inc(idx_ready, 1)
                    group(GROUPS, slot_of(GROUPS), GROUPS // S, RAGGED, general, False)

                for s in range(S):
                    indices(s, s, 0)
                spread = v.value_load(flag[:], min_val=0, max_val=1)
                with v.If(spread < 1):
                    all_groups(False)
                with v.Else():
                    all_groups(True)
                norm_coefficients(v, stats[:], z_counted, GROUPS + 1, gb[:, 0:1], gb[:, 1:2], bn1,
                                  tmp, pair_ps, aggr, paired, rooted, bn1_steps)

        stage = ExitStack()
        with stage:
            def sb(name, shape, dt=F32):
                return stage.enter_context(nc.sbuf_tensor(name, shape, dt))

            S = 4
            s_buf = [sb(f"s_buf{s}", [P, CHUNK, HALF]) for s in range(S)]
            s_buf_r = sb("s_buf_r", [P, T_HALF])
            stats = sb("stats2", [P, GROUPS + 1, 6])
            z_loaded = [sem(f"z_loaded{s}") for s in range(S)]
            s_stored = [sem(f"s_stored{s}") for s in range(S)]
            r_loaded, r_stored, gated, s_counted = sem("r_loaded"), sem("r_stored"), sem("gated"), sem("s_counted")
            aggr, paired, rooted = sem("aggr2"), sem("paired2"), sem("rooted2")
            bn2_steps = sem("bn2_steps")

            def chunk_of(mem, c):
                return mem[bass.ds(c, 1)].rearrange("a p k w -> (a p) k w")

            blk = stage.enter_context(nc.Block())

            @blk.sync
            def _(sp):
                def load(c, s, turn):
                    after(sp, s_stored[s], 16 * turn)
                    sp.dma_start(s_buf[s][:], chunk_of(edge_mem, c)).then_inc(z_loaded[s], 16)
                rounds(sp, CHUNKS, S, load)
                sp.dma_start(s_buf_r[:], edge_mem_r).then_inc(r_loaded, 16)

            @blk.scalar
            def _(act):
                def gate(c, s, turn):
                    act.wait_ge(z_loaded[s], 16 * turn + 16)
                    act.activation(s_buf[s][:], s_buf[s][:], ACT.Sigmoid, scale=bn1[:, 0:1], bias=bn1[:, 1:2]).then_inc(gated, 1)
                rounds(act, CHUNKS, S, gate)
                act.wait_ge(r_loaded, 16)
                act.activation(s_buf_r[:], s_buf_r[:], ACT.Sigmoid, scale=bn1[:, 0:1], bias=bn1[:, 1:2]).then_inc(gated, 1)
                act.wait_ge(aggr, 3)
                act.activation(tmp[:, 7:8], tmp[:, 6:7], ACT.Sqrt).then_inc(rooted, 1)

            @blk.gpsimd
            def _(gp):
                def store(c, s, turn):
                    gp.wait_ge(s_counted, c + 1)
                    gp.dma_start(chunk_of(edge_mem, c), s_buf[s][:]).then_inc(s_stored[s], 16)
                rounds(gp, CHUNKS, S, store)
                gp.wait_ge(gated, CHUNKS + 1)
                gp.dma_start(edge_mem_r, s_buf_r[:]).then_inc(r_stored, 16)
                for s in range(S):
                    gp.wait_ge(s_stored[s], 16 * (CHUNKS // S + (s < CHUNKS % S)))
                gp.wait_ge(r_stored, 16)

            @blk.vector
            def _(v):
                def count(c, s, turn):
                    v.wait_ge(gated, c + 1)
                    for k in range(CHUNK):
                        ins = v.bn_stats(stats[:, bass.ds(c * CHUNK + k, 1), :].rearrange("p a k -> p (a k)"), s_buf[s][:, k, :])
                    ins.then_inc(s_counted, 1)
                rounds(v, CHUNKS, S, count)
                v.wait_ge(gated, CHUNKS + 1)
                v.bn_stats(stats[:, GROUPS, :], s_buf_r[:]).then_inc(s_counted, 1)
                norm_coefficients(v, stats[:], s_counted, CHUNKS + 1, gb[:, 2:3], gb[:, 3:4], bn2,
                                  tmp, pair_ps, aggr, paired, rooted, bn2_steps)

            @blk.tensor
            def _(pe):
                pe.wait_ge(aggr, 1)
                pe.matmul(pair_ps[:, 0:1], fold[:], tmp[:, 0:1], start=True, stop=True).then_inc(paired, 1)
                pe.wait_ge(aggr, 2)
                pe.matmul(pair_ps[:, 1:2], fold[:], tmp[:, 4:5], start=True, stop=True).then_inc(paired, 1)

        agg = keep("agg", [P, N_PAD])
        stage = ExitStack()
        with stage:
            def sb(name, shape, dt=F32):
                return stage.enter_context(nc.sbuf_tensor(name, shape, dt))

            S = 2
            s_in = [sb(f"s_in{s}", [P, CHUNK, HALF]) for s in range(S)]
            h_buf = [sb(f"h_buf{s}", [P, CHUNK, HALF]) for s in range(S)]
            lin = [sb(f"lin{s}", [P, CHUNK, HALF]) for s in range(S)]
            h_rows = [sb(f"h_rows{k}", [P, TILES, P]) for k in range(CHUNK)]
            near = [sb(f"near{k}", [P, 2 * TILES, WIN]) for k in range(CHUNK)]
            win_rel = sb("win_rel", [P, 2 * TILES])
            turn_ps = [stage.enter_context(nc.psum_tensor(f"turn_ps{k}", [P, TILES, P], F32)) for k in range(CHUNK)]
            sum_ps = [stage.enter_context(nc.psum_tensor(f"sum_ps{k}", [P, WIN], F32)) for k in range(CHUNK)]

            s_loaded = [sem(f"s_loaded{s}") for s in range(S)]
            cleared, raised, capped, logged, lined, maxed, h_ready = (
                sem(n) for n in ("cleared", "raised", "capped", "logged", "lined", "maxed", "h_ready"))
            win_summed, turned, rows_ready, near_ready, summed, added, rel_made = (
                sem(n) for n in ("win_summed", "turned", "rows_ready", "near_ready", "summed", "added", "rel_made"))

            blk = stage.enter_context(nc.Block())

            def all_chunks(eng, body):
                rounds(eng, CHUNKS, S, lambda c, s, turn: body(c, s, turn, FULL, CHUNK))
                body(CHUNKS, CHUNKS % S, CHUNKS // S, RAGGED, 1)

            def cols(buf, size):
                return buf[:] if size is FULL else buf[:, 0, 0:size.half]

            @blk.sync
            def _(sp):
                def load(c, s, turn, size, groups):
                    after(sp, h_ready, c - S + 1)
                    after(sp, lined, c - S + 1)
                    sp.dma_start(cols(s_in[s], size), chunk_of(edge_mem, c) if size is FULL else edge_mem_r).then_inc(s_loaded[s], 16)
                all_chunks(sp, load)

            @blk.scalar
            def _(act):
                def soft(c, s, turn, size, groups):
                    act.wait_ge(s_loaded[s], 16 * turn + 16)
                    after(act, turned, (c - S) * CHUNK + CHUNK)
                    act.activation(cols(h_buf[s], size), cols(s_in[s], size), ACT.Exp, scale=bn2[:, 0:1], bias=bn2[:, 1:2]).then_inc(raised, 1)
                    act.wait_ge(capped, c + 1)
                    act.activation(cols(h_buf[s], size), cols(h_buf[s], size), ACT.Ln, bias=1.0).then_inc(logged, 1)

                def turn_out(c, size, groups):
                    for k in range(groups):
                        g = c * CHUNK + k
                        act.wait_ge(turned, g + 1)
                        after(act, summed, g - CHUNK + 1)
                        act.activation(h_rows[k][0:size.tile, 0:size.tiles, :], turn_ps[k][0:size.tile, 0:size.tiles, :], ACT.Copy).then_inc(rows_ready, 1)

                soft(0, 0, 0, FULL, CHUNK)
                soft(1, 1, 0, FULL, CHUNK)
                turn_out(0, FULL, CHUNK)
                with act.Fori(1, CHUNKS // S) as i:
                    for s in range(S):
                        soft(i * S + s, s, i, FULL, CHUNK)
                        turn_out(i * S + s - 1, FULL, CHUNK)
                soft(CHUNKS - 1, 0, CHUNKS // S, FULL, CHUNK)
                turn_out(CHUNKS - 2, FULL, CHUNK)
                soft(CHUNKS, 1, CHUNKS // S, RAGGED, 1)
                turn_out(CHUNKS - 1, FULL, CHUNK)
                turn_out(CHUNKS, RAGGED, 1)

            @blk.gpsimd
            def _(gp):
                gp.memset(agg[:], 0.0).then_inc(cleared, 1)

                def multiply(c, s, turn, size, groups):
                    gp.wait_ge(maxed, c + 1)
                    gp.tensor_tensor(cols(h_buf[s], size), cols(h_buf[s], size), cols(s_in[s], size), ALU.mult).then_inc(h_ready, 1)
                all_chunks(gp, multiply)

            @blk.tensor
            def _(pe):
                def segments(c, s, turn, size, groups, general):
                    pe.wait_ge(h_ready, c + 1)
                    for k in range(groups):
                        g = c * CHUNK + k
                        after(pe, rows_ready, g - CHUNK + 1)
                        for t in range(size.tiles):
                            mm = pe.transpose(turn_ps[k][0:size.tile, t, :], h_buf[s][:, k, t * size.tile:(t + 1) * size.tile], ident[:])
                        mm.then_inc(turned, 1)

                    def window_sums(k):
                        for h in range(2):
                            for t in range(size.tiles):
                                mm = pe.matmul(sum_ps[k][h * F:(h + 1) * F, :], h_rows[k][0:size.tile, t, h * F:(h + 1) * F],
                                               near[k][0:size.tile, h * size.tiles + t, :], start=(t == 0), stop=(t == size.tiles - 1))
                        return mm

                    for k in range(groups):
                        g = c * CHUNK + k
                        pe.wait_ge(rows_ready, g + 1)
                        if not general:
                            pe.wait_ge(near_ready, g + 1)
                            after(pe, added, g - CHUNK + 1)
                            window_sums(k).then_inc(summed, 1)
                        else:
                            pe.sem_inc(sweep_on, 1)
                            with pe.Fori(0, WINDOWS) as w:
                                pe.wait_ge(near_ready, g * WINDOWS + w + 1)
                                window_sums(k).then_inc(win_summed, 1)
                            pe.wait_ge(win_summed, (g + 1) * WINDOWS)
                            pe.sem_inc(summed, 1)

                spread = pe.value_load(flag[:], min_val=0, max_val=1)
                with pe.If(spread < 1):
                    all_chunks(pe, lambda *a: segments(*a, False))
                with pe.Else():
                    all_chunks(pe, lambda *a: segments(*a, True))
                pe.nop()

            @blk.vector
            def _(v):
                def soft(c, s, turn, size, groups):
                    v.wait_ge(raised, c + 1)
                    v.tensor_scalar(cols(h_buf[s], size), cols(h_buf[s], size), EXP_CAP, None, ALU.min).then_inc(capped, 1)
                    after(v, maxed, c - S + 1)
                    v.tensor_scalar(cols(lin[s], size), cols(s_in[s], size), bn2[:, 0:1], bn2[:, 1:2], ALU.mult, ALU.add).then_inc(lined, 1)

                def top(c, s, turn, size, groups):
                    v.wait_ge(logged, c + 1)
                    v.wait_ge(lined, c + 1)
                    v.tensor_tensor(cols(h_buf[s], size), cols(h_buf[s], size), cols(lin[s], size), ALU.max).then_inc(maxed, 1)

                def match(k, size, rel_of):
                    n = 2 * size.tiles
                    return v.tensor_tensor(near[k][0:size.tile, 0:n, :],
                                           iota_row[0:size.tile, :].rearrange("p (a n) -> p a n", a=1).broadcast_to([size.tile, n, WIN]),
                                           rel_of.rearrange("p (j a) -> p j a", a=1).broadcast_to([size.tile, n, WIN]), ALU.is_equal)

                def dst_of(table, table_r, g, size):
                    if size is FULL:
                        return table[:, bass.ds(g, 1), :, :].rearrange("p g h t -> p (g h t)")
                    return table_r[:].rearrange("p h t -> p (h t)")

                def hots(c, size, groups):
                    for k in range(groups):
                        g = c * CHUNK + k
                        after(v, summed, g - CHUNK + 1)
                        match(k, size, dst_of(rel, rel_r, g, size)).then_inc(near_ready, 1)

                def add(k, h, base):
                    lanes = agg[h * F:(h + 1) * F, bass.ds(base, WIN)]
                    return v.tensor_tensor(lanes, lanes, sum_ps[k][h * F:(h + 1) * F, :], ALU.add)

                def sums(c, size, groups, general):
                    for k in range(groups):
                        g = c * CHUNK + k
                        if not general:
                            bases = [v.value_load(base_s[:, bass.ds(g * 2 + h, 1)], min_val=0, max_val=N_PAD - WIN) for h in range(2)]
                            v.wait_ge(summed, g + 1)
                            after(v, added, g)
                            add(k, 0, bases[0])
                            add(k, 1, bases[1]).then_inc(added, 1)
                        else:
                            with v.Fori(0, WINDOWS) as w:
                                v.wait_ge(added, g * WINDOWS + w + 1)
                                v.tensor_scalar(win_rel[0:size.tile, 0:2 * size.tiles], dst_of(dst_tf, dst_rf, g, size),
                                                win_start[0:size.tile, bass.ds(w, 1)], None, ALU.subtract).then_inc(rel_made, 1)
                                v.wait_ge(rel_made, g * WINDOWS + w + 1)
                                match(k, size, win_rel[0:size.tile, 0:2 * size.tiles]).then_inc(near_ready, 1)
                                v.wait_ge(win_summed, g * WINDOWS + w + 1)
                                add(k, 0, w * WIN)
                                add(k, 1, w * WIN).then_inc(added, 1)

                def all_of_it(general):
                    def ahead(c, s, turn, size, groups):
                        soft(c, s, turn, size, groups)
                        if not general:
                            hots(c, size, groups)
                        top(c, s, turn, size, groups)

                    ahead(0, 0, 0, FULL, CHUNK)
                    soft_next = ahead
                    soft_next(1, 1, 0, FULL, CHUNK) if general else None
                    if general:
                        sums(0, FULL, CHUNK, True)
                        with v.Fori(1, CHUNKS // S) as i:
                            for s in range(S):
                                ahead(i * S + s, s, i, FULL, CHUNK)
                                sums(i * S + s - 1, FULL, CHUNK, True)
                        ahead(CHUNKS - 1, 0, CHUNKS // S, FULL, CHUNK)
                        sums(CHUNKS - 2, FULL, CHUNK, True)
                        ahead(CHUNKS, 1, CHUNKS // S, RAGGED, 1)
                        sums(CHUNKS - 1, FULL, CHUNK, True)
                        sums(CHUNKS, RAGGED, 1, True)
                        return
                    def step(c, s, turn, size, groups):
                        soft(c, s, turn, size, groups)
                        sums(c - 1, FULL, CHUNK, False)
                        hots(c, size, groups)
                        top(c, s, turn, size, groups)
                    step(1, 1, 0, FULL, CHUNK)
                    with v.Fori(1, CHUNKS // S) as i:
                        for s in range(S):
                            step(i * S + s, s, i, FULL, CHUNK)
                    step(CHUNKS - 1, 0, CHUNKS // S, FULL, CHUNK)
                    step(CHUNKS, 1, CHUNKS // S, RAGGED, 1)
                    sums(CHUNKS, RAGGED, 1, False)

                v.wait_ge(cleared, 1)
                spread = v.value_load(flag[:], min_val=0, max_val=1)
                with v.If(spread < 1):
                    all_of_it(False)
                with v.Else():
                    v.sem_inc(added, 1)
                    all_of_it(True)
                v.nop()

        stage = ExitStack()
        with stage:
            def sb(name, shape, dt=F32):
                return stage.enter_context(nc.sbuf_tensor(name, shape, dt))

            S = 2
            COLS = 500
            PARTS = N_NODES // COLS
            NB = BLOCK * F
            x_sb = sb("x_sb", [P, WINDOWS, F])
            y = sb("y", [P, WINDOWS, F])
            scaled = sb("scaled", [P, F])
            shifts = sb("shifts", [F, F])
            ones_f = sb("ones_f", [F, P])
            shift_all = sb("shift_all", [P, F])
            stats = sb("stats3", [P, PARTS, 6])
            ln = sb("ln", [P, WINDOWS, 6])
            mean, var, dif = (sb(n, [P, WINDOWS]) for n in ("mean", "var", "dif"))
            fold_ps = [stage.enter_context(nc.psum_tensor(f"fold_ps{s}", [P, 512], F32)) for s in range(S)]
            y_ps = [stage.enter_context(nc.psum_tensor(f"y_ps{s}", [P, BLOCK, F], F32)) for s in range(S)]
            shift_ps = stage.enter_context(nc.psum_tensor("shift_ps", [P, F], F32))

            x_in4, folded, f_counted, aggr, paired, rooted, bn3_steps = (
                sem(n) for n in ("x_in4", "folded", "f_counted", "aggr3", "paired3", "rooted3", "bn3_steps"))
            coefs, shifted, y_ready, y_added, ln_steps, ln_root, ln_rooted, normed, stored = (
                sem(n) for n in ("coefs", "shifted", "y_ready", "y_added", "ln_steps", "ln_root", "ln_rooted", "normed", "stored"))

            blk = stage.enter_context(nc.Block())

            @blk.sync
            def _(sp):
                sp.dma_start(x_sb[:].rearrange("p t f -> p (t f)"), x_nodes).then_inc(x_in4, 16)
                for n in range(2):
                    half = slice(n * WINDOWS // 2, (n + 1) * WINDOWS // 2)
                    sp.wait_ge(normed, n + 1)
                    sp.dma_start(out.rearrange("p (t f) -> p t f", f=F)[:, half, :], y[:, half, :]).then_inc(stored, 16)
                sp.wait_ge(stored, 32)

            @blk.gpsimd
            def _(gp):
                gp.memset(ones_f[:], 1.0).then_inc(coefs, 1)

            @blk.tensor
            def _(pe):
                for n in range(PARTS):
                    after(pe, f_counted, n - S + 1)
                    pe.matmul(fold_ps[n % S][:, 0:COLS], fold[:], agg[:, n * COLS:(n + 1) * COLS], start=True, stop=True).then_inc(folded, 1)
                pe.wait_ge(aggr, 1)
                pe.matmul(pair_ps[:, 0:1], fold[:], tmp[:, 0:1], start=True, stop=True).then_inc(paired, 1)
                pe.wait_ge(aggr, 2)
                pe.matmul(pair_ps[:, 1:2], fold[:], tmp[:, 4:5], start=True, stop=True).then_inc(paired, 1)
                pe.wait_ge(coefs, 3)
                pe.matmul(shift_ps[:], ones_f[:], shifts[:], start=True, stop=True).then_inc(shifted, 1)
                by_tile = agg[:].rearrange("k (p t) -> k t p", t=WINDOWS)
                for n in range(BLOCKS):
                    after(pe, y_added, n - S + 1)
                    for b in range(BLOCK):
                        mm = pe.matmul(y_ps[n % S][:, b, :], by_tile[:, n * BLOCK + b, :], scaled[:], start=True, stop=True)
                    mm.then_inc(y_ready, 1)

            @blk.scalar
            def _(act):
                act.wait_ge(aggr, 3)
                act.activation(tmp[:, 7:8], tmp[:, 6:7], ACT.Sqrt).then_inc(rooted, 1)
                act.wait_ge(ln_root, 1)
                act.activation(dif[:], var[:], ACT.Sqrt).then_inc(ln_rooted, 1)

            @blk.vector
            def _(v):
                for n in range(PARTS):
                    v.wait_ge(folded, n + 1)
                    v.bn_stats(stats[:, n, :], fold_ps[n % S][:, 0:COLS]).then_inc(f_counted, 1)
                norm_coefficients(v, stats[:], f_counted, PARTS, gb[:, 4:5], gb[:, 5:6], bn3,
                                  tmp, pair_ps, aggr, paired, rooted, bn3_steps)
                v.tensor_scalar(scaled[:], fold[:, 0:F], bn3[:, 0:1], None, ALU.mult).then_inc(coefs, 1)
                v.tensor_scalar(shifts[:], ident[0:F, 0:F], bn3[0:F, 1:2], None, ALU.mult).then_inc(coefs, 1)
                v.wait_ge(shifted, 1)
                v.tensor_copy(shift_all[:], shift_ps[:]).then_inc(ln_steps, 1)
                v.wait_ge(x_in4, 16)
                v.wait_ge(ln_steps, 1)
                v.scalar_tensor_tensor(out=y[:], in0=x_sb[:], scalar=2.0,
                                       in1=shift_all[:].rearrange("p (a f) -> p a f", a=1).broadcast_to([P, WINDOWS, F]),
                                       op0=ALU.mult, op1=ALU.add).then_inc(ln_steps, 1)
                v.wait_ge(ln_steps, 2)
                for n in range(BLOCKS):
                    v.wait_ge(y_ready, n + 1)
                    part = y[:, n * BLOCK:(n + 1) * BLOCK, :]
                    v.tensor_tensor(part, part, y_ps[n % S][:], ALU.add).then_inc(y_added, 1)
                v.wait_ge(y_added, BLOCKS)
                for t in range(WINDOWS):
                    ins = v.bn_stats(ln[:, t, :], y[:, t, :])
                ins.then_inc(ln_steps, 1)
                n = [3]

                def step(ins):
                    n[0] += 1
                    ins.then_inc(ln_steps, 1)
                    v.wait_ge(ln_steps, n[0])

                v.wait_ge(ln_steps, 3)
                step(v.tensor_tensor(mean[:], ln[:, :, 1], ln[:, :, 4], ALU.add))
                step(v.tensor_scalar(mean[:], mean[:], 0.5, None, ALU.mult))
                step(v.tensor_tensor(dif[:], ln[:, :, 1], mean[:], ALU.subtract))
                step(v.tensor_tensor(dif[:], dif[:], dif[:], ALU.mult))
                step(v.tensor_tensor(var[:], ln[:, :, 2], ln[:, :, 5], ALU.add))
                step(v.tensor_scalar(var[:], var[:], 1.0 / F, EPS, ALU.mult, ALU.add))
                step(v.tensor_tensor(var[:], var[:], dif[:], ALU.add))
                v.sem_inc(ln_root, 1)
                v.wait_ge(ln_rooted, 1)
                step(v.reciprocal(var[:], dif[:]))
                for half in range(2):
                    at = slice(half * WINDOWS // 2, (half + 1) * WINDOWS // 2)
                    shape = [P, WINDOWS // 2, F]
                    step(v.tensor_tensor(y[:, at, :], y[:, at, :], mean[:, at].rearrange("p (t a) -> p t a", a=1).broadcast_to(shape), ALU.subtract))
                    v.tensor_tensor(y[:, at, :], y[:, at, :], var[:, at].rearrange("p (t a) -> p t a", a=1).broadcast_to(shape), ALU.mult).then_inc(normed, 1)



def norm_coefficients(v, stats, counted, count, gamma, beta, coef, tmp, pair_ps, aggr, paired, rooted, steps):
    n = [0]

    def step(ins):
        n[0] += 1
        ins.then_inc(steps, 1)
        v.wait_ge(steps, n[0])

    v.wait_ge(counted, count)
    step(v.bn_aggr(tmp[:, 0:2], stats))
    v.sem_inc(aggr, 1)
    v.wait_ge(paired, 1)
    step(v.tensor_scalar(tmp[:, 2:3], pair_ps[:, 0:1], 0.5, None, ALU.mult))
    step(v.tensor_tensor(tmp[:, 3:4], tmp[:, 0:1], tmp[:, 2:3], ALU.subtract))
    step(v.tensor_tensor(tmp[:, 3:4], tmp[:, 3:4], tmp[:, 3:4], ALU.mult))
    step(v.tensor_tensor(tmp[:, 4:5], tmp[:, 1:2], tmp[:, 3:4], ALU.add))
    v.sem_inc(aggr, 1)
    v.wait_ge(paired, 2)
    step(v.tensor_scalar(tmp[:, 6:7], pair_ps[:, 1:2], 0.5, EPS, ALU.mult, ALU.add))
    v.sem_inc(aggr, 1)
    v.wait_ge(rooted, 1)
    step(v.reciprocal(tmp[:, 8:9], tmp[:, 7:8]))
    step(v.tensor_tensor(coef[:, 0:1], tmp[:, 8:9], gamma, ALU.mult))
    step(v.tensor_tensor(tmp[:, 9:10], tmp[:, 2:3], coef[:, 0:1], ALU.mult))
    step(v.tensor_tensor(coef[:, 1:2], beta, tmp[:, 9:10], ALU.subtract))


def kernel(**inputs):
    import concourse.bacc as bacc
    from concourse.bass_utils import run_bass_kernel_spmd

    a = {k: np.asarray(v) for k, v in inputs.items()}
    x, src, dst, e = a["x"], a["src"], a["dst"], a["edge_attr_41"]
    w1 = a["L0_gnn_W1"]
    x_pad = np.zeros((N_PAD, F), x.dtype)
    x_pad[:N_NODES] = x
    xt = x_pad.reshape(P, BLOCKS, BLOCK, F).transpose(1, 3, 2, 0)

    def by_tile(v):
        return v[:MAIN].reshape(GROUPS, 2, TILES, P).transpose(3, 0, 1, 2), v[MAIN:].reshape(2, T_TILES, T_P).transpose(2, 0, 1)

    src_t, src_r = by_tile(src)
    dst_t, dst_r = by_tile(dst)
    e_main = np.zeros((GROUPS, 2, E_ROWS, HALF), e.dtype)
    e_main[:, :, :EDGE_F] = e[:MAIN].reshape(GROUPS, 2, HALF, EDGE_F).transpose(0, 1, 3, 2)
    e_ragged = np.zeros((2, E_ROWS, T_HALF), e.dtype)
    e_ragged[:, :EDGE_F] = e[MAIN:].reshape(2, T_HALF, EDGE_F).transpose(0, 2, 1)
    w_nodes = np.concatenate([w1[:, :F].T, w1[:, F:2 * F].T], axis=1)
    w_edges = np.zeros((2, E_ROWS, 2, F), w1.dtype)
    for h in range(2):
        w_edges[h, :EDGE_F, h] = w1[:, 2 * F:].T
    arrays = {
        "xt": xt, "x_nodes": x_pad.reshape(P, WINDOWS * F),
        "src_t": src_t.reshape(P, GROUPS, 2 * TILES), "src_r": src_r.reshape(T_P, 2 * T_TILES),
        "dst_t": dst_t, "dst_r": dst_r, "dst_h": dst[:MAIN].reshape(D_ROWS, D_HALVES, HALF),
        "dst_hr": dst[MAIN:].reshape(2, T_HALF),
        "e_main": e_main.reshape(GROUPS, 2 * E_ROWS, HALF), "e_ragged": e_ragged.reshape(2 * E_ROWS, T_HALF),
        "w_nodes": w_nodes, "w_edges": w_edges.reshape(2 * E_ROWS, P), "b1": a["L0_gnn_b1"],
        "g1": a["L0_gnn_g1"], "bt1": a["L0_gnn_bt1"], "g2": a["L0_gnn_g2"], "bt2": a["L0_gnn_bt2"],
        "g3": a["L0_gnn_g3"], "bt3": a["L0_gnn_bt3"],
    }
    arrays = {k: np.ascontiguousarray(v) for k, v in arrays.items()}
    nc = bacc.Bacc("TRN2", target_bir_lowering=False, num_devices=1)
    args = [nc.dram_tensor(k, v.shape, mybir.dt.from_np(v.dtype), kind="ExternalInput").ap() for k, v in arrays.items()]
    out = nc.dram_tensor("out", (P, WINDOWS * F), F32, kind="ExternalOutput").ap()
    build(nc, *args, out)
    r = run_bass_kernel_spmd(nc, [arrays], core_ids=[0])
    return np.asarray(r.results[0]["out"]).reshape(N_PAD, F)[:N_NODES]
```

```python
import numpy as np
import concourse.bass as bass
from concourse import mybir
from contextlib import ExitStack

F32 = mybir.dt.float32
I32 = mybir.dt.int32
ALU = mybir.AluOpType
ACT = mybir.ActivationFunctionType
AX = mybir.AxisListType

N_NODES, N_EDGES, F, EDGE_F = 12500, 200000, 64, 41
EPS = 1e-5

P = 128
HALF = 512
TILES = HALF // P
GROUPS = N_EDGES // (2 * HALF)
CHUNK = 3
CHUNKS = GROUPS // CHUNK
WIDE = CHUNK * HALF
T_HALF = (N_EDGES - GROUPS * 2 * HALF) // 2
T_P = 80
T_TILES = T_HALF // T_P
HALVES = 2 * GROUPS + 2
MAIN = GROUPS * 2 * HALF

NODE_TILES = -(-N_NODES // P)
N_PAD = NODE_TILES * P
WIN = 98
WINDOWS = N_PAD // WIN
BLOCK = 7
BLOCKS = NODE_TILES // BLOCK

E_ROWS = 48
D_ROWS, D_HALVES = 78, 5
EXP_CAP = 1e18


class Halves:

    def __init__(self, half, tile):
        self.half, self.tile, self.tiles = half, tile, half // tile


FULL, RAGGED = Halves(HALF, P), Halves(T_HALF, T_P)


def after(eng, sem, count):
    if isinstance(count, int) and count <= 0:
        return
    eng.wait_ge(sem, count)


def rounds(eng, total, slots, body):
    for s in range(slots):
        body(s, s, 0)
    turns = total // slots
    with eng.Fori(1, turns) as i:
        for s in range(slots):
            body(i * slots + s, s, i)
    for s in range(total - turns * slots):
        body(turns * slots + s, s, turns)


class Item:

    def __init__(self, c, slot, turn):
        self.c, self.slot, self.turn = c, slot, turn
        ragged = isinstance(c, int) and c == CHUNKS
        self.size, self.groups = (RAGGED, 1) if ragged else (FULL, CHUNK)

    def cols(self, buf):
        return buf[:] if self.size is FULL else buf[:, 0, 0:self.size.half]


def pipeline(eng, slots, lag, body):
    def step(t, s, turn):
        def back(k):
            c = t - k
            if isinstance(c, int) and not 0 <= c <= CHUNKS:
                return None
            return Item(c, (s - k) % slots, turn + (s - k) // slots)
        body(back)

    turns = CHUNKS // slots
    for t in range(2 * slots):
        step(t, t % slots, t // slots)
    with eng.Fori(2, turns) as i:
        for s in range(slots):
            step(i * slots + s, s, i)
    for t in range(turns * slots, CHUNKS + 1 + lag):
        step(t, t % slots, t // slots)


def build(nc, xt, x_nodes, src_t, src_r, dst_t, dst_r, dst_h, dst_hr, e_main, e_ragged,
          x, w_dst, w_src, w_edges, b1, g1, bt1, g2, bt2, g3, bt3, out):
    ctx = ExitStack()
    with ctx:
        def dram(name, shape, dt=F32):
            return nc.dram_tensor(name, shape, dt, kind="Internal").ap()

        q_table = dram("q_table", [N_PAD, F])
        dst_f = dram("dst_f", [1, N_EDGES])
        base_f = dram("base_f", [1, HALVES])
        base_i = dram("base_i", [1, HALVES], I32)
        reach = dram("reach", [1, HALVES])
        edge_mem = dram("edge_mem", [GROUPS, P, HALF])
        edge_mem_r = dram("edge_mem_r", [P, T_HALF])

        def keep(name, shape, dt=F32):
            return ctx.enter_context(nc.sbuf_tensor(name, shape, dt))

        def sem(name):
            return ctx.enter_context(nc.semaphore(name))

        def chunk_of(c):
            return edge_mem[bass.ds(c * CHUNK, CHUNK)].rearrange("k p w -> p k w")

        ident = keep("ident", [P, P])
        fold = keep("fold", [P, P])
        base_s = keep("base_s", [1, HALVES], I32)
        base_all = keep("base_all", [P, HALVES])
        flag = keep("flag", [1, 1], I32)
        rel = keep("rel", [P, GROUPS, 2 * TILES])
        rel_r = keep("rel_r", [T_P, 2 * T_TILES])
        dst_tf = keep("dst_tf", [P, GROUPS, 2 * TILES])
        dst_rf = keep("dst_rf", [T_P, 2 * T_TILES])
        iota_row = keep("iota_row", [P, WIN])
        gb = keep("gb", [P, 6])
        bn1 = keep("bn1", [P, 2])
        bn2 = keep("bn2", [P, 2])
        bn3 = keep("bn3", [P, 2])
        tmp = keep("tmp", [P, 12])
        bumps = sem("bumps")

        stage = ExitStack()
        with stage:
            def sb(name, shape, dt=F32):
                return stage.enter_context(nc.sbuf_tensor(name, shape, dt))

            S = 4
            src_idx = sb("src_idx", [P, GROUPS, 2 * TILES], I32)
            src_idx_r = sb("src_idx_r", [T_P, 2 * T_TILES], I32)
            idx = [sb(f"idx{s}", [P, 2 * TILES], I32) for s in range(S)]
            rows = [sb(f"rows{s}", [P, TILES, 2, F]) for s in range(S)]
            xg = [sb(f"xg{s}", [P, HALF]) for s in range(2)]
            e_in = [sb(f"e_in{s}", [2 * E_ROWS, HALF]) for s in range(S)]
            q_in = [sb(f"q_in{s}", [WIN, 2, F]) for s in range(S)]
            d_in = [sb(f"d_in{s}", [1, 2, HALF]) for s in range(S)]
            z_sb = [sb(f"z_sb{s}", [P, HALF]) for s in range(S)]
            hot = sb("hot", [WIN, 2, HALF])
            qw_in = sb("qw_in", [WIN, F])
            w_edge = sb("w_edge", [2 * E_ROWS, P])
            w_rows = sb("w_rows", [P, P])
            w_q = sb("w_q", [F, F])
            b1_all = sb("b1_all", [P, F])
            ones = sb("ones", [1, P])
            stats = sb("stats", [P, GROUPS + 1, 6])
            x_in = [sb(f"x_in{s}", [F, BLOCK, P]) for s in range(2)]
            q_out = [sb(f"q_out{s}", [P, BLOCK, F]) for s in range(2)]
            dst_hi = sb("dst_hi", [D_ROWS, D_HALVES, HALF], I32)
            dst_hf = sb("dst_hf", [D_ROWS, D_HALVES, HALF])
            dst_ri = sb("dst_ri", [2, 1, T_HALF], I32)
            dst_rrf = sb("dst_rrf", [2, 1, T_HALF])
            low = sb("low", [D_ROWS, 3, D_HALVES])
            low_r = sb("low_r", [2, 3, 1])
            low_i = sb("low_i", [D_ROWS, D_HALVES], I32)
            low_ri = sb("low_ri", [2, 1], I32)
            reach_row = sb("reach_row", [1, HALVES])
            farthest = sb("farthest", [1, 2])
            iota_p = sb("iota_p", [P, 1])
            node_col = sb("node_col", [P, HALVES])
            win_col = sb("win_col", [P, WINDOWS])
            z_ps = [stage.enter_context(nc.psum_tensor(f"z_ps{s}", [P, HALF], F32)) for s in range(2)]
            xg_ps = [stage.enter_context(nc.psum_tensor(f"xg_ps{s}", [P, HALF], F32)) for s in range(2)]
            d_ps = stage.enter_context(nc.psum_tensor("d_ps", [P, 2, HALF], F32))
            q_ps = [stage.enter_context(nc.psum_tensor(f"q_ps{s}", [P, 8, F], F32)) for s in range(2)]
            pair = q_ps[0][:, 0, :]

            src_in, dst_in, w_in, w_in2 = sem("src_in"), sem("dst_in"), sem("w_in"), sem("w_in2")
            x_loaded = [sem(f"x_loaded{s}") for s in range(2)]
            q_stored = [sem(f"q_stored{s}") for s in range(2)]
            projected, q_biased = sem("projected"), sem("q_biased")
            dst_cast, lows, bases_out, bases_in, flag_set = (sem(n) for n in ("dst_cast", "lows", "bases_out", "bases_in", "flag_set"))
            made, masks, prep = sem("made"), sem("masks"), sem("prep")
            loaded = [sem(f"loaded{s}") for s in range(S)]
            q_loaded = [sem(f"q_loaded{s}") for s in range(S)]
            gathered = [sem(f"gathered{s}") for s in range(S)]
            z_stored = [sem(f"z_stored{s}") for s in range(S)]
            idx_ready, turned, xg_ready, dst_spread, hot_ready = (
                sem(n) for n in ("idx_ready", "turned", "xg_ready", "dst_spread", "hot_ready"))
            z_ready, z_copied, z_counted = sem("z_ready"), sem("z_copied"), sem("z_counted")
            win_loaded, win_hot, win_used = sem("win_loaded"), sem("win_hot"), sem("win_used")
            aggr, paired, rooted, bn1_steps = sem("aggr"), sem("paired"), sem("rooted"), sem("bn1_steps")
            R_SLOT, R_TURN = GROUPS % S, GROUPS // S

            blk = stage.enter_context(nc.Block())

            @blk.sync
            def _(sp):
                sp.dma_start(src_idx[:], src_t).then_inc(src_in, 16)
                sp.dma_start(dst_hi[:], dst_h).then_inc(dst_in, 16)
                sp.dma_start(dst_ri[:], dst_hr).then_inc(dst_in, 16)
                sp.dma_start(w_q[:], w_dst).then_inc(w_in, 16)
                sp.dma_start(b1_all[:], b1.partition_broadcast(P)).then_inc(w_in, 16)
                for n in range(2):
                    sp.dma_start(x_in[n][:], xt[n]).then_inc(x_loaded[n], 16)
                sp.dma_start(src_idx_r[:], src_r).then_inc(w_in2, 16)
                sp.dma_start(w_rows[:], w_src).then_inc(w_in2, 16)
                sp.dma_start(w_edge[:], w_edges).then_inc(w_in2, 16)
                for n, v in enumerate((g1, bt1, g2, bt2, g3, bt3)):
                    for h in range(2):
                        sp.dma_start(gb[h * F:(h + 1) * F, n:n + 1], v.rearrange("(f a) -> f a", a=1)).then_inc(w_in2, 16)
                for n in range(2, BLOCKS):
                    sp.wait_ge(projected, n - 1)
                    sp.dma_start(x_in[n % 2][:], xt[n]).then_inc(x_loaded[n % 2], 16)
                sp.wait_ge(dst_cast, 2)
                sp.dma_start(dst_f[:, 0:MAIN].rearrange("a (p w) -> (a p) w", p=D_ROWS),
                             dst_hf[:].rearrange("p h w -> p (h w)")).then_inc(bases_out, 16)
                sp.dma_start(dst_f[:, MAIN:].rearrange("a (p w) -> (a p) w", p=2), dst_rrf[:, 0, :]).then_inc(bases_out, 16)
                sp.wait_ge(lows, 1)
                for row, main, ragged in ((base_f, low[:, 0, :], low_r[:, 0, :]), (base_i, low_i[:], low_ri[:]),
                                          (reach, low[:, 2, :], low_r[:, 2, :])):
                    sp.dma_start(row[:, 0:2 * GROUPS].rearrange("a (p h) -> (a p) h", p=D_ROWS), main).then_inc(bases_out, 16)
                    sp.dma_start(row[:, 2 * GROUPS:].rearrange("a (p h) -> (a p) h", p=2), ragged).then_inc(bases_out, 16)
                sp.wait_ge(bases_out, 8 * 16)
                sp.dma_start(base_s[:], base_i).then_inc(bases_in, 16)
                sp.dma_start(reach_row[:], reach).then_inc(bases_in, 16)
                sp.dma_start(base_all[:], base_f.rearrange("a h -> (a h)").partition_broadcast(P)).then_inc(bases_in, 16)

                def load(g, s, size, general):
                    after(sp, z_ready, g - S + 1)
                    if size is FULL:
                        sp.dma_start(e_in[s][:], e_main[bass.ds(g, 1)].rearrange("a r w -> (a r) w")).then_inc(loaded[s], 16)
                    else:
                        sp.dma_start(e_in[s][:, 0:size.half], e_ragged).then_inc(loaded[s], 16)
                    sp.dma_start(d_in[s][:, :, 0:size.half],
                                 dst_f[:, bass.ds(g * 2 * HALF, 2 * size.half)].rearrange("a (h w) -> a h w", h=2)).then_inc(loaded[s], 16)
                    if not general:
                        for h in range(2):
                            base = sp.value_load(base_s[:, bass.ds(g * 2 + h, 1)], min_val=0, max_val=N_PAD - WIN)
                            sp.dma_start(q_in[s][:, h, :], q_table[bass.ds(base, WIN), :]).then_inc(q_loaded[s], 16)
                    else:
                        with sp.Fori(0, WINDOWS) as w:
                            sp.wait_ge(win_used, g * WINDOWS + w + 1)
                            sp.dma_start(qw_in[:], q_table[bass.ds(w * WIN, WIN), :]).then_inc(win_loaded, 16)

                def all_groups(general):
                    rounds(sp, GROUPS, S, lambda g, s, turn: load(g, s, FULL, general))
                    load(GROUPS, R_SLOT, RAGGED, general)

                for s in range(2):
                    sp.wait_ge(q_stored[s], 16 * (BLOCKS // 2))
                sp.wait_ge(flag_set, 1)
                spread = sp.value_load(flag[:], min_val=0, max_val=1)
                with sp.If(spread < 1):
                    all_groups(False)
                with sp.Else():
                    all_groups(True)
                sp.nop()

            @blk.gpsimd
            def _(gp):
                def gather(g, s, size):
                    gp.wait_ge(idx_ready, g + 1)
                    after(gp, turned, g - S + 1)
                    gp.sem_inc(bumps, 1)
                    for t in range(size.tiles):
                        for h in range(2):
                            j = h * size.tiles + t
                            gp.indirect_dma_start(out=rows[s][0:size.tile, t, h, :], out_offset=None, in_=x,
                                                  in_offset=bass.IndirectOffsetOnAxis(ap=idx[s][0:size.tile, j:j + 1], axis=0)
                                                  ).then_inc(gathered[s], 16)

                for t in (ident, fold):
                    gp.memset(t[:], 0.0).then_inc(masks, 1)
                gp.memset(ones[:], 1.0).then_inc(made, 1)
                gp.iota(iota_row[:], [[1, WIN]], base=0, channel_multiplier=0, allow_small_or_imprecise_dtypes=True).then_inc(made, 1)
                gp.iota(iota_p[:], [[0, 1]], base=0, channel_multiplier=1, allow_small_or_imprecise_dtypes=True).then_inc(made, 1)
                gp.iota(win_col[:], [[WIN, WINDOWS]], base=0, channel_multiplier=1, allow_small_or_imprecise_dtypes=True).then_inc(made, 1)
                for n, (t, off) in enumerate(((ident, 0), (fold, 0), (fold, -F), (fold, F))):
                    gp.wait_ge(masks, 2 + n)
                    gp.affine_select(out=t[:], in_=t[:], compare_op=ALU.not_equal, fill=1.0, base=off,
                                     pattern=[[-1, P]], channel_multiplier=1).then_inc(masks, 1)
                rounds(gp, GROUPS, S, lambda g, s, turn: gather(g, s, FULL))
                gather(GROUPS, R_SLOT, RAGGED)

            @blk.tensor
            def _(pe):
                pe.wait_ge(w_in, 32)
                for n in range(BLOCKS):
                    pe.wait_ge(x_loaded[n % 2], 16 * (n // 2 + 1))
                    after(pe, q_biased, n - 1)
                    for b in range(BLOCK):
                        mm = pe.matmul(q_ps[n % 2][:, b, :], x_in[n % 2][:, b, :], w_q[:], start=True, stop=True)
                    mm.then_inc(projected, 1)
                pe.wait_ge(w_in2, 15 * 16)
                pe.wait_ge(made, 4)
                pe.wait_ge(masks, 6)

                def group(g, s, turn, size, general):
                    w = size.half
                    pe.wait_ge(loaded[s], 32 * turn + 32)
                    after(pe, hot_ready, g)
                    for h in range(2):
                        mm = pe.matmul(d_ps[0:WIN, h, 0:w], ones[:, 0:WIN], d_in[s][:, h, 0:w], start=True, stop=True)
                    mm.then_inc(dst_spread, 1)
                    pe.wait_ge(gathered[s], turn * 2 * TILES * 16 + 2 * size.tiles * 16)
                    after(pe, xg_ready, g - 1)
                    for t in range(size.tiles):
                        mm = pe.transpose(xg_ps[s % 2][:, t * size.tile:(t + 1) * size.tile],
                                          rows[s][0:size.tile, t, :, :].rearrange("p h f -> p (h f)"), ident[0:size.tile, 0:size.tile])
                    mm.then_inc(turned, 1)
                    after(pe, z_copied, g - 1)
                    pe.matmul(z_ps[s % 2][:, 0:w], w_edge[:], e_in[s][:, 0:w], start=True, stop=False)

                    def windows(which, last):
                        for h in range(2):
                            mm = pe.matmul(z_ps[s % 2][h * F:(h + 1) * F, 0:w], which(h), hot[:, h, 0:w], start=False, stop=last)
                        return mm

                    pe.wait_ge(xg_ready, g + 1)
                    if not general:
                        pe.matmul(z_ps[s % 2][:, 0:w], w_rows[:], xg[s % 2][:, 0:w], start=False, stop=False)
                        pe.wait_ge(q_loaded[s], 32 * turn + 32)
                        pe.wait_ge(hot_ready, g + 1)
                        windows(lambda h: q_in[s][:, h, :], True).then_inc(z_ready, 1)
                    else:
                        pe.sem_inc(bumps, 1)
                        with pe.Fori(0, WINDOWS) as k:
                            pe.wait_ge(win_loaded, (g * WINDOWS + k + 1) * 16)
                            pe.wait_ge(win_hot, g * WINDOWS + k + 1)
                            windows(lambda h: qw_in[:], False).then_inc(win_used, 1)
                        pe.matmul(z_ps[s % 2][:, 0:w], w_rows[:], xg[s % 2][:, 0:w], start=False, stop=True).then_inc(z_ready, 1)

                def all_groups(general):
                    rounds(pe, GROUPS, S, lambda g, s, turn: group(g, s, turn, FULL, general))
                    group(GROUPS, R_SLOT, R_TURN, RAGGED, general)

                pe.wait_ge(flag_set, 1)
                spread = pe.value_load(flag[:], min_val=0, max_val=1)
                with pe.If(spread < 1):
                    all_groups(False)
                with pe.Else():
                    pe.sem_inc(win_used, 1)
                    all_groups(True)
                pair_sums(pe, fold, tmp, pair, aggr, paired)

            @blk.scalar
            def _(act):
                q_view = q_table.rearrange("(p n b) f -> n p b f", p=P, b=BLOCK)
                for n in range(BLOCKS):
                    act.wait_ge(q_biased, n + 1)
                    act.dma_start(q_view[n], q_out[n % 2][:]).then_inc(q_stored[n % 2], 16)

                def copy_rows(g, s, size):
                    act.wait_ge(turned, g + 1)
                    after(act, z_ready, g - 1)
                    act.activation(xg[s % 2][:, 0:size.half], xg_ps[s % 2][:, 0:size.half], ACT.Copy).then_inc(xg_ready, 1)

                def copy_z(g, s, turn, size):
                    act.wait_ge(z_ready, g + 1)
                    after(act, z_counted, g - S + 1)
                    after(act, z_stored[s], 16 * turn)
                    act.activation(z_sb[s][:, 0:size.half], z_ps[s % 2][:, 0:size.half], ACT.Copy).then_inc(z_copied, 1)
                    act.wait_ge(z_copied, g + 1)
                    to = edge_mem[bass.ds(g, 1)].rearrange("a p w -> (a p) w") if size is FULL else edge_mem_r
                    act.dma_start(to, z_sb[s][:, 0:size.half]).then_inc(z_stored[s], 16)

                def both(g, s, turn, size):
                    copy_rows(g, s, size)
                    copy_z(g, s, turn, size)
                rounds(act, GROUPS, S, lambda g, s, turn: both(g, s, turn, FULL))
                both(GROUPS, R_SLOT, R_TURN, RAGGED)
                for s in range(S):
                    act.wait_ge(z_stored[s], 16 * (GROUPS // S + (s <= R_SLOT)))
                act.wait_ge(aggr, 3)
                act.activation(tmp[:, 7:8], tmp[:, 6:7], ACT.Sqrt).then_inc(rooted, 1)

            @blk.vector
            def _(v):
                def indices(g, s):
                    v.tensor_copy(idx[s][:], src_idx[:, bass.ds(g, 1), :].rearrange("p a j -> p (a j)")).then_inc(idx_ready, 1)

                v.wait_ge(src_in, 16)
                for s in range(S):
                    indices(s, s)
                v.wait_ge(dst_in, 32)
                v.tensor_copy(dst_hf[:], dst_hi[:]).then_inc(dst_cast, 1)
                v.tensor_copy(dst_rrf[:], dst_ri[:]).then_inc(dst_cast, 1)
                v.wait_ge(dst_cast, 2)
                for wide, lo in ((dst_hf, low), (dst_rrf, low_r)):
                    v.tensor_reduce(lo[:, 0, :], wide[:], AX.X, ALU.min).then_inc(prep, 1)
                    v.tensor_reduce(lo[:, 1, :], wide[:], AX.X, ALU.max).then_inc(prep, 1)
                v.wait_ge(prep, 4)
                for lo in (low, low_r):
                    v.tensor_scalar(lo[:, 0, :], lo[:, 0, :], float(N_PAD - WIN), None, ALU.min).then_inc(prep, 1)
                v.wait_ge(prep, 6)
                for lo, lo_i in ((low, low_i), (low_r, low_ri)):
                    v.tensor_copy(lo_i[:], lo[:, 0, :]).then_inc(prep, 1)
                    v.tensor_tensor(lo[:, 2, :], lo[:, 1, :], lo[:, 0, :], ALU.subtract).then_inc(prep, 1)
                v.wait_ge(prep, 10)
                v.sem_inc(lows, 1)

                for n in range(BLOCKS):
                    v.wait_ge(projected, n + 1)
                    after(v, q_stored[n % 2], 16 * (n // 2))
                    v.tensor_tensor(q_out[n % 2][:], q_ps[n % 2][:, 0:BLOCK, :],
                                    b1_all[:].rearrange("p (a f) -> p a f", a=1).broadcast_to([P, BLOCK, F]), ALU.add).then_inc(q_biased, 1)

                v.wait_ge(bases_in, 48)
                v.wait_ge(made, 4)
                v.tensor_reduce(farthest[:, 0:1], reach_row[:], AX.X, ALU.max).then_inc(prep, 1)
                v.tensor_scalar(node_col[:], base_all[:], iota_p[:], None, ALU.add).then_inc(prep, 1)
                v.wait_ge(prep, 12)
                v.tensor_scalar(farthest[:, 1:2], farthest[:, 0:1], float(WIN), None, ALU.is_ge).then_inc(prep, 1)
                v.wait_ge(prep, 13)
                v.tensor_copy(flag[:], farthest[:, 1:2]).then_inc(flag_set, 1)

                def group(g, s, size, general, more):
                    v.wait_ge(dst_spread, g + 1)
                    after(v, z_ready, g)
                    if not general:
                        for h in range(2):
                            hots = v.tensor_scalar(hot[:, h, 0:size.half], d_ps[0:WIN, h, 0:size.half],
                                                   node_col[0:WIN, bass.ds(g * 2 + h, 1)], None, ALU.is_equal)
                        hots.then_inc(hot_ready, 1)
                    else:
                        v.sem_inc(bumps, 1)
                        with v.Fori(0, WINDOWS) as k:
                            v.wait_ge(win_used, g * WINDOWS + k + 1)
                            for h in range(2):
                                hots = v.tensor_scalar(hot[:, h, 0:size.half], d_ps[0:WIN, h, 0:size.half],
                                                       win_col[0:WIN, bass.ds(k, 1)], None, ALU.is_equal)
                            hots.then_inc(win_hot, 1)
                        v.wait_ge(win_hot, g * WINDOWS + WINDOWS)
                        v.sem_inc(hot_ready, 1)
                    v.wait_ge(z_copied, g + 1)
                    v.bn_stats(stats[:, bass.ds(g, 1), :].rearrange("p a k -> p (a k)"), z_sb[s][:, 0:size.half]).then_inc(z_counted, 1)
                    if more:
                        indices(g + S, s)

                def all_groups(general):
                    for g in range(S):
                        group(g, g, FULL, general, True)
                    with v.Fori(1, GROUPS // S - 1) as i:
                        for s in range(S):
                            group(i * S + s, s, FULL, general, True)
                    for g in range(S * (GROUPS // S - 1), GROUPS):
                        group(g, g % S, FULL, general, g + S < GROUPS)
                        if g + S == GROUPS:
                            v.tensor_copy(idx[g % S][0:T_P, 0:2 * T_TILES], src_idx_r[:]).then_inc(idx_ready, 1)
                    group(GROUPS, R_SLOT, RAGGED, general, False)

                v.wait_ge(flag_set, 1)
                v.wait_ge(w_in2, 15 * 16)
                spread = v.value_load(flag[:], min_val=0, max_val=1)
                with v.If(spread < 1):
                    all_groups(False)
                with v.Else():
                    all_groups(True)
                norm_coefficients(v, stats[:], z_counted, GROUPS + 1, gb[:, 0:1], gb[:, 1:2], bn1,
                                  tmp, pair, aggr, paired, rooted, bn1_steps)

        stage = ExitStack()
        with stage:
            def sb(name, shape, dt=F32):
                return stage.enter_context(nc.sbuf_tensor(name, shape, dt))

            S = 4
            s_buf = [sb(f"s_buf{s}", [P, CHUNK, HALF]) for s in range(S)]
            s_buf_r = sb("s_buf_r", [P, T_HALF])
            stats = sb("stats2", [P, GROUPS + 1, 6])
            dst_ti = sb("dst_ti", [P, GROUPS, 2 * TILES], I32)
            dst_tri = sb("dst_tri", [T_P, 2 * T_TILES], I32)
            pair_ps = stage.enter_context(nc.psum_tensor("pair_ps", [P, 512], F32))
            z_loaded = [sem(f"z_loaded{s}") for s in range(S)]
            s_stored = [sem(f"s_stored{s}") for s in range(S)]
            r_loaded, r_stored, gated, s_counted = sem("r_loaded"), sem("r_stored"), sem("gated"), sem("s_counted")
            tiles_in, tiles_cast = sem("tiles_in"), sem("tiles_cast")
            aggr, paired, rooted, bn2_steps = sem("aggr2"), sem("paired2"), sem("rooted2"), sem("bn2_steps")

            blk = stage.enter_context(nc.Block())

            @blk.sync
            def _(sp):
                def load(c, s, turn):
                    after(sp, s_stored[s], 16 * turn)
                    sp.dma_start(s_buf[s][:], chunk_of(c)).then_inc(z_loaded[s], 16)
                rounds(sp, CHUNKS, S, load)
                sp.dma_start(s_buf_r[:], edge_mem_r).then_inc(r_loaded, 16)
                sp.dma_start(dst_ti[:], dst_t).then_inc(tiles_in, 16)
                sp.dma_start(dst_tri[:], dst_r).then_inc(tiles_in, 16)

            @blk.scalar
            def _(act):
                def gate(c, s, turn):
                    act.wait_ge(z_loaded[s], 16 * turn + 16)
                    act.activation(s_buf[s][:], s_buf[s][:], ACT.Sigmoid, scale=bn1[:, 0:1], bias=bn1[:, 1:2]).then_inc(gated, 1)
                rounds(act, CHUNKS, S, gate)
                act.wait_ge(r_loaded, 16)
                act.activation(s_buf_r[:], s_buf_r[:], ACT.Sigmoid, scale=bn1[:, 0:1], bias=bn1[:, 1:2]).then_inc(gated, 1)
                act.wait_ge(aggr, 3)
                act.activation(tmp[:, 7:8], tmp[:, 6:7], ACT.Sqrt).then_inc(rooted, 1)

            @blk.gpsimd
            def _(gp):
                def store(c, s, turn):
                    gp.wait_ge(s_counted, c + 1)
                    gp.dma_start(chunk_of(c), s_buf[s][:]).then_inc(s_stored[s], 16)
                rounds(gp, CHUNKS, S, store)
                gp.wait_ge(gated, CHUNKS + 1)
                gp.dma_start(edge_mem_r, s_buf_r[:]).then_inc(r_stored, 16)
                for s in range(S):
                    gp.wait_ge(s_stored[s], 16 * (CHUNKS // S + (s < CHUNKS % S)))
                gp.wait_ge(r_stored, 16)

            @blk.vector
            def _(v):
                def count(c, s, turn):
                    v.wait_ge(gated, c + 1)
                    for k in range(CHUNK):
                        ins = v.bn_stats(stats[:, bass.ds(c * CHUNK + k, 1), :].rearrange("p a k -> p (a k)"), s_buf[s][:, k, :])
                    ins.then_inc(s_counted, 1)
                rounds(v, CHUNKS, S, count)
                v.wait_ge(gated, CHUNKS + 1)
                v.bn_stats(stats[:, GROUPS, :], s_buf_r[:]).then_inc(s_counted, 1)
                norm_coefficients(v, stats[:], s_counted, CHUNKS + 1, gb[:, 2:3], gb[:, 3:4], bn2,
                                  tmp, pair_ps, aggr, paired, rooted, bn2_steps)
                v.wait_ge(tiles_in, 32)
                v.tensor_copy(dst_tf[:], dst_ti[:]).then_inc(tiles_cast, 1)
                v.tensor_copy(dst_rf[:], dst_tri[:]).then_inc(tiles_cast, 1)
                v.wait_ge(tiles_cast, 2)
                v.tensor_tensor(rel[:].rearrange("p g (h t) -> p g h t", h=2), dst_tf[:].rearrange("p g (h t) -> p g h t", h=2),
                                base_all[:, 0:2 * GROUPS].rearrange("p (g h a) -> p g h a", h=2, a=1).broadcast_to([P, GROUPS, 2, TILES]), ALU.subtract)
                v.tensor_tensor(rel_r[:].rearrange("p (h t) -> p h t", h=2), dst_rf[:].rearrange("p (h t) -> p h t", h=2),
                                base_all[0:T_P, 2 * GROUPS:].rearrange("p (h a) -> p h a", a=1).broadcast_to([T_P, 2, T_TILES]), ALU.subtract)

            @blk.tensor
            def _(pe):
                pair_sums(pe, fold, tmp, pair_ps, aggr, paired)

        agg = keep("agg", [P, N_PAD])
        stage = ExitStack()
        with stage:
            def sb(name, shape, dt=F32):
                return stage.enter_context(nc.sbuf_tensor(name, shape, dt))

            S = 4
            LAG = 4
            s_in = [sb(f"s_in{s}", [P, CHUNK, HALF]) for s in range(S)]
            h_buf = [sb(f"h_buf{s}", [P, CHUNK, HALF]) for s in range(S)]
            lin = [sb(f"lin{s}", [P, CHUNK, HALF]) for s in range(2)]
            h_rows = [sb(f"h_rows{s}", [P, CHUNK, TILES, P]) for s in range(2)]
            near = [sb(f"near{s}", [P, CHUNK * 2 * TILES, WIN]) for s in range(2)]
            win_start = sb("win_start", [P, WINDOWS])
            win_rel = sb("win_rel", [P, 2 * TILES])
            turn_ps = stage.enter_context(nc.psum_tensor("turn_ps", [P, CHUNK, TILES, P], F32))
            sum_ps = [stage.enter_context(nc.psum_tensor(f"sum_ps{k}", [P, 512], F32)) for k in range(CHUNK)]

            s_loaded = [sem(f"s_loaded{s}") for s in range(S)]
            cleared, raised, capped, logged, lined, maxed, h_ready = (
                sem(n) for n in ("cleared", "raised", "capped", "logged", "lined", "maxed", "h_ready"))
            h_turned, rows_ready, near_ready, summed, added, rel_made, win_near, win_summed, win_added = (
                sem(n) for n in ("h_turned", "rows_ready", "near_ready", "summed", "added", "rel_made", "win_near", "win_summed", "win_added"))

            blk = stage.enter_context(nc.Block())

            @blk.sync
            def _(sp):
                def step(back):
                    if m := back(0):
                        after(sp, h_ready, m.c - S + 1)
                        sp.dma_start(m.cols(s_in[m.slot]), chunk_of(m.c) if m.size is FULL else edge_mem_r).then_inc(s_loaded[m.slot], 16)
                pipeline(sp, S, 0, step)

            @blk.scalar
            def _(act):
                act.preload_act_table_set("natural_log_exp_and_others")

                def step(back):
                    if m := back(1):
                        act.wait_ge(capped, m.c + 1)
                        act.activation(m.cols(h_buf[m.slot]), m.cols(h_buf[m.slot]), ACT.Ln, bias=1.0).then_inc(logged, 1)
                    if m := back(0):
                        act.wait_ge(s_loaded[m.slot], 16 * m.turn + 16)
                        after(act, h_turned, m.c - S + 1)
                        act.activation(m.cols(h_buf[m.slot]), m.cols(s_in[m.slot]), ACT.Exp, scale=bn2[:, 0:1], bias=bn2[:, 1:2]).then_inc(raised, 1)
                        after(act, maxed, m.c - 1)
                        act.activation(m.cols(lin[m.slot % 2]), m.cols(s_in[m.slot]), ACT.Identity, scale=bn2[:, 0:1], bias=bn2[:, 1:2]).then_inc(lined, 1)
                    if m := back(2):
                        act.wait_ge(h_turned, m.c + 1)
                        after(act, summed, m.c - 1)
                        at = (slice(0, m.size.tile), slice(0, m.groups), slice(0, m.size.tiles))
                        act.activation(h_rows[m.slot % 2][at], turn_ps[at], ACT.Copy).then_inc(rows_ready, 1)
                pipeline(act, S, 2, step)

            @blk.gpsimd
            def _(gp):
                gp.memset(agg[:], 0.0).then_inc(cleared, 1)
                gp.iota(win_start[:], [[WIN, WINDOWS]], base=0, channel_multiplier=0, allow_small_or_imprecise_dtypes=True).then_inc(cleared, 1)

                def step(back):
                    if m := back(0):
                        gp.wait_ge(raised, m.c + 1)
                        gp.sem_inc(bumps, 1)
                        gp.tensor_scalar(m.cols(h_buf[m.slot]), m.cols(h_buf[m.slot]), EXP_CAP, None, ALU.min).then_inc(capped, 1)
                    if m := back(1):
                        gp.wait_ge(maxed, m.c + 1)
                        gp.tensor_tensor(m.cols(h_buf[m.slot]), m.cols(h_buf[m.slot]), m.cols(s_in[m.slot]), ALU.mult).then_inc(h_ready, 1)
                pipeline(gp, S, 1, step)

            @blk.tensor
            def _(pe):
                def window_sums(m, k):
                    n = m.size
                    for h in range(2):
                        for t in range(n.tiles):
                            mm = pe.matmul(sum_ps[k][h * F:(h + 1) * F, 0:WIN], h_rows[m.slot % 2][0:n.tile, k, t, h * F:(h + 1) * F],
                                           near[m.slot % 2][0:n.tile, (2 * k + h) * n.tiles + t, :], start=(t == 0), stop=(t == n.tiles - 1))
                    return mm

                def step(back, general):
                    if m := back(2):
                        pe.wait_ge(h_ready, m.c + 1)
                        after(pe, rows_ready, m.c)
                        for k in range(m.groups):
                            for t in range(m.size.tiles):
                                mm = pe.transpose(turn_ps[0:m.size.tile, k, t, :], h_buf[m.slot][:, k, t * m.size.tile:(t + 1) * m.size.tile], ident[:])
                        mm.then_inc(h_turned, 1)
                    if m := back(3):
                        pe.wait_ge(rows_ready, m.c + 1)
                        if not general:
                            pe.wait_ge(near_ready, m.c + 1)
                            after(pe, added, m.c)
                            for k in range(m.groups):
                                mm = window_sums(m, k)
                            mm.then_inc(summed, 1)
                        else:
                            for k in range(m.groups):
                                pe.sem_inc(bumps, 1)
                                with pe.Fori(0, WINDOWS) as w:
                                    pe.wait_ge(win_near, (m.c * CHUNK + k) * WINDOWS + w + 1)
                                    window_sums(m, k).then_inc(win_summed, 1)
                            pe.wait_ge(win_summed, (m.c * CHUNK + m.groups) * WINDOWS)
                            pe.sem_inc(summed, 1)

                spread = pe.value_load(flag[:], min_val=0, max_val=1)
                with pe.If(spread < 1):
                    pipeline(pe, S, 3, lambda back: step(back, False))
                with pe.Else():
                    pipeline(pe, S, 3, lambda back: step(back, True))
                pe.nop()

            @blk.vector
            def _(v):
                def match(out_of, n, rel_of):
                    rows = out_of.shape[0]
                    return v.tensor_tensor(out_of, iota_row[0:rows, :].rearrange("p (a n) -> p a n", a=1).broadcast_to([rows, n, WIN]),
                                           rel_of.rearrange("p (j a) -> p j a", a=1).broadcast_to([rows, n, WIN]), ALU.is_equal)

                def dst_of(m, table, table_r, first, groups):
                    if m.size is RAGGED:
                        return table_r[:]
                    return table[:, bass.ds(m.c * CHUNK + first, groups), :].rearrange("p g j -> p (g j)")

                def add(k, h, base):
                    lanes = agg[h * F:(h + 1) * F, bass.ds(base, WIN)]
                    return v.tensor_tensor(lanes, lanes, sum_ps[k][h * F:(h + 1) * F, 0:WIN], ALU.add)

                def top(m):
                    v.wait_ge(logged, m.c + 1)
                    v.wait_ge(lined, m.c + 1)
                    v.tensor_tensor(m.cols(h_buf[m.slot]), m.cols(h_buf[m.slot]), m.cols(lin[m.slot % 2]), ALU.max).then_inc(maxed, 1)

                def step(back):
                    if m := back(4):
                        for k in range(m.groups):
                            g = m.c * CHUNK + k
                            bases = [v.value_load(base_s[:, bass.ds(g * 2 + h, 1)], min_val=0, max_val=N_PAD - WIN) for h in range(2)]
                            if k == 0:
                                v.wait_ge(summed, m.c + 1)
                            after(v, win_added, g)
                            add(k, 0, bases[0])
                            ins = add(k, 1, bases[1]).then_inc(win_added, 1)
                        v.wait_ge(win_added, m.c * CHUNK + m.groups)
                        v.sem_inc(added, 1)
                    if m := back(1):
                        top(m)
                    if m := back(2):
                        after(v, summed, m.c - 1)
                        n = m.groups * 2 * m.size.tiles
                        match(near[m.slot % 2][0:m.size.tile, 0:n, :], n, dst_of(m, rel, rel_r, 0, CHUNK)).then_inc(near_ready, 1)

                def step_general(back):
                    if m := back(1):
                        top(m)
                    if m := back(3):
                        n = 2 * m.size.tiles
                        part = win_rel[0:m.size.tile, 0:n]
                        for k in range(m.groups):
                            g = m.c * CHUNK + k
                            with v.Fori(0, WINDOWS) as w:
                                v.wait_ge(win_added, g * WINDOWS + w + 1)
                                v.tensor_scalar(part, dst_of(m, dst_tf, dst_rf, k, 1), win_start[0:m.size.tile, bass.ds(w, 1)],
                                                None, ALU.subtract).then_inc(rel_made, 1)
                                v.wait_ge(rel_made, g * WINDOWS + w + 1)
                                match(near[m.slot % 2][0:m.size.tile, k * n:(k + 1) * n, :], n, part).then_inc(win_near, 1)
                                v.wait_ge(win_summed, g * WINDOWS + w + 1)
                                add(k, 0, w * WIN)
                                add(k, 1, w * WIN).then_inc(win_added, 1)

                v.wait_ge(cleared, 2)
                spread = v.value_load(flag[:], min_val=0, max_val=1)
                with v.If(spread < 1):
                    pipeline(v, S, 4, step)
                with v.Else():
                    v.sem_inc(win_added, 1)
                    pipeline(v, S, 4, step_general)
                v.nop()

        stage = ExitStack()
        with stage:
            def sb(name, shape, dt=F32):
                return stage.enter_context(nc.sbuf_tensor(name, shape, dt))

            S = 2
            COLS = 500
            PARTS = N_NODES // COLS
            SHARES = 2
            SHARE = NODE_TILES // SHARES
            x_sb = sb("x_sb", [P, NODE_TILES, F])
            y = sb("y", [P, NODE_TILES, F])
            scaled = sb("scaled", [P, F])
            shifts = sb("shifts", [F, F])
            ones_f = sb("ones_f", [F, P])
            stats = sb("stats3", [P, PARTS, 6])
            ln = sb("ln", [P, NODE_TILES, 6])
            mean, var, dif = (sb(n, [P, NODE_TILES]) for n in ("mean", "var", "dif"))
            fold_ps = [stage.enter_context(nc.psum_tensor(f"fold_ps{s}", [P, 512], F32)) for s in range(S)]
            y_ps = [stage.enter_context(nc.psum_tensor(f"y_ps{s}", [P, 8, F], F32)) for s in range(S)]
            pair_ps = stage.enter_context(nc.psum_tensor("pair_ps4", [P, 512], F32))

            x_in4, folded, f_counted, aggr, paired, rooted, bn3_steps = (
                sem(n) for n in ("x_in4", "folded", "f_counted", "aggr3", "paired3", "rooted3", "bn3_steps"))
            coefs, doubled, y_ready, y_added, y_counted, ln_steps, ln_root, ln_rooted, normed, stored = (
                sem(n) for n in ("coefs", "doubled", "y_ready", "y_added", "y_counted", "ln_steps", "ln_root", "ln_rooted", "normed", "stored"))

            blk = stage.enter_context(nc.Block())

            @blk.sync
            def _(sp):
                sp.dma_start(x_sb[:].rearrange("p t f -> p (t f)"), x_nodes).then_inc(x_in4, 16)
                for n in range(SHARES):
                    share = slice(n * SHARE, (n + 1) * SHARE)
                    sp.wait_ge(normed, n + 1)
                    sp.dma_start(out.rearrange("p (t f) -> p t f", f=F)[:, share, :], y[:, share, :]).then_inc(stored, 16)
                sp.wait_ge(stored, 16 * SHARES)

            @blk.gpsimd
            def _(gp):
                gp.memset(ones_f[:], 1.0).then_inc(coefs, 1)

            @blk.tensor
            def _(pe):
                for n in range(PARTS):
                    after(pe, f_counted, n - S + 1)
                    pe.matmul(fold_ps[n % S][:, 0:COLS], fold[:], agg[:, n * COLS:(n + 1) * COLS], start=True, stop=True).then_inc(folded, 1)
                pair_sums(pe, fold, tmp, pair_ps, aggr, paired)
                pe.wait_ge(coefs, 3)
                by_tile = agg[:].rearrange("k (p t) -> k t p", t=NODE_TILES)
                for n in range(BLOCKS):
                    after(pe, y_added, n - S + 1)
                    for b in range(BLOCK):
                        pe.matmul(y_ps[n % S][:, b, :], by_tile[:, n * BLOCK + b, :], scaled[:], start=True, stop=False)
                        mm = pe.matmul(y_ps[n % S][:, b, :], ones_f[:], shifts[:], start=False, stop=True)
                    mm.then_inc(y_ready, 1)

            @blk.scalar
            def _(act):
                act.wait_ge(x_in4, 16)
                act.activation(y[:], x_sb[:], ACT.Copy, scale=2.0).then_inc(doubled, 1)
                act.wait_ge(aggr, 3)
                act.activation(tmp[:, 7:8], tmp[:, 6:7], ACT.Sqrt).then_inc(rooted, 1)
                act.wait_ge(ln_root, 1)
                act.activation(dif[:], var[:], ACT.Sqrt).then_inc(ln_rooted, 1)

            @blk.vector
            def _(v):
                for n in range(PARTS):
                    v.wait_ge(folded, n + 1)
                    v.bn_stats(stats[:, n, :], fold_ps[n % S][:, 0:COLS]).then_inc(f_counted, 1)
                norm_coefficients(v, stats[:], f_counted, PARTS, gb[:, 4:5], gb[:, 5:6], bn3,
                                  tmp, pair_ps, aggr, paired, rooted, bn3_steps)
                v.tensor_scalar(scaled[:], fold[:, 0:F], bn3[:, 0:1], None, ALU.mult).then_inc(coefs, 1)
                v.tensor_scalar(shifts[:], ident[0:F, 0:F], bn3[0:F, 1:2], None, ALU.mult).then_inc(coefs, 1)
                v.wait_ge(doubled, 1)

                def join(n, s, turn):
                    part = y[:, bass.ds(n * BLOCK, BLOCK), :]
                    v.wait_ge(y_ready, n + 1)
                    v.tensor_tensor(part, part, y_ps[s][:, 0:BLOCK, :], ALU.add).then_inc(y_added, 1)
                    v.wait_ge(y_added, n + 1)
                    for b in range(BLOCK):
                        t = n * BLOCK + b
                        ins = v.bn_stats(ln[:, bass.ds(t, 1), :].rearrange("p a k -> p (a k)"), y[:, bass.ds(t, 1), :].rearrange("p a f -> p (a f)"))
                    ins.then_inc(y_counted, 1)
                rounds(v, BLOCKS, S, join)
                n = [0]

                def step(ins):
                    n[0] += 1
                    ins.then_inc(ln_steps, 1)
                    v.wait_ge(ln_steps, n[0])

                v.wait_ge(y_counted, BLOCKS)
                step(v.tensor_tensor(mean[:], ln[:, :, 1], ln[:, :, 4], ALU.add))
                step(v.tensor_scalar(mean[:], mean[:], 0.5, None, ALU.mult))
                step(v.tensor_tensor(dif[:], ln[:, :, 1], mean[:], ALU.subtract))
                step(v.tensor_tensor(dif[:], dif[:], dif[:], ALU.mult))
                step(v.tensor_tensor(var[:], ln[:, :, 2], ln[:, :, 5], ALU.add))
                step(v.tensor_scalar(var[:], var[:], 1.0 / F, EPS, ALU.mult, ALU.add))
                step(v.tensor_tensor(var[:], var[:], dif[:], ALU.add))
                v.sem_inc(ln_root, 1)
                v.wait_ge(ln_rooted, 1)
                step(v.reciprocal(var[:], dif[:]))
                for share in range(SHARES):
                    with v.Fori(0, SHARE // BLOCK) as i:
                        for b in range(BLOCK):
                            t = i * BLOCK + (share * SHARE + b)
                            tile = y[:, bass.ds(t, 1), :].rearrange("p a f -> p (a f)")
                            ins = v.tensor_scalar(tile, tile, mean[:, bass.ds(t, 1)], var[:, bass.ds(t, 1)], ALU.subtract, ALU.mult)
                        ins.then_inc(ln_steps, 1)
                    n[0] += SHARE // BLOCK
                    v.wait_ge(ln_steps, n[0])
                    v.sem_inc(normed, 1)


def pair_sums(pe, fold, tmp, pair, aggr, paired):
    pe.wait_ge(aggr, 1)
    pe.matmul(pair[:, 0:1], fold[:], tmp[:, 0:1], start=True, stop=True).then_inc(paired, 1)
    pe.wait_ge(aggr, 2)
    pe.matmul(pair[:, 1:2], fold[:], tmp[:, 4:5], start=True, stop=True).then_inc(paired, 1)


def norm_coefficients(v, stats, counted, count, gamma, beta, coef, tmp, pair, aggr, paired, rooted, steps):
    n = [0]

    def step(ins):
        n[0] += 1
        ins.then_inc(steps, 1)
        v.wait_ge(steps, n[0])

    v.wait_ge(counted, count)
    step(v.bn_aggr(tmp[:, 0:2], stats))
    v.sem_inc(aggr, 1)
    v.wait_ge(paired, 1)
    step(v.tensor_scalar(tmp[:, 2:3], pair[:, 0:1], 0.5, None, ALU.mult))
    step(v.tensor_tensor(tmp[:, 3:4], tmp[:, 0:1], tmp[:, 2:3], ALU.subtract))
    step(v.tensor_tensor(tmp[:, 3:4], tmp[:, 3:4], tmp[:, 3:4], ALU.mult))
    step(v.tensor_tensor(tmp[:, 4:5], tmp[:, 1:2], tmp[:, 3:4], ALU.add))
    v.sem_inc(aggr, 1)
    v.wait_ge(paired, 2)
    step(v.tensor_scalar(tmp[:, 6:7], pair[:, 1:2], 0.5, EPS, ALU.mult, ALU.add))
    v.sem_inc(aggr, 1)
    v.wait_ge(rooted, 1)
    step(v.reciprocal(tmp[:, 8:9], tmp[:, 7:8]))
    step(v.tensor_tensor(coef[:, 0:1], tmp[:, 8:9], gamma, ALU.mult))
    step(v.tensor_tensor(tmp[:, 9:10], tmp[:, 2:3], coef[:, 0:1], ALU.mult))
    step(v.tensor_tensor(coef[:, 1:2], beta, tmp[:, 9:10], ALU.subtract))


def kernel(**inputs):
    import concourse.bacc as bacc
    from concourse.bass_utils import run_bass_kernel_spmd

    a = {k: np.asarray(v) for k, v in inputs.items()}
    x, src, dst, e = a["x"], a["src"], a["dst"], a["edge_attr_41"]
    w1 = a["L0_gnn_W1"]
    x_pad = np.zeros((N_PAD, F), x.dtype)
    x_pad[:N_NODES] = x
    xt = x_pad.reshape(P, BLOCKS, BLOCK, F).transpose(1, 3, 2, 0)

    def by_tile(v):
        return v[:MAIN].reshape(GROUPS, 2, TILES, P).transpose(3, 0, 1, 2), v[MAIN:].reshape(2, T_TILES, T_P).transpose(2, 0, 1)

    src_t, src_r = by_tile(src)
    dst_t, dst_r = by_tile(dst)
    e_main = np.zeros((GROUPS, 2, E_ROWS, HALF), e.dtype)
    e_main[:, :, :EDGE_F] = e[:MAIN].reshape(GROUPS, 2, HALF, EDGE_F).transpose(0, 1, 3, 2)
    e_ragged = np.zeros((2, E_ROWS, T_HALF), e.dtype)
    e_ragged[:, :EDGE_F] = e[MAIN:].reshape(2, T_HALF, EDGE_F).transpose(0, 2, 1)
    w_src = np.zeros((2, F, 2, F), w1.dtype)
    w_edges = np.zeros((2, E_ROWS, 2, F), w1.dtype)
    for h in range(2):
        w_edges[h, :EDGE_F, h] = w1[:, 2 * F:].T
        w_src[h, :, h] = w1[:, :F].T
    arrays = {
        "xt": xt, "x_nodes": x_pad.reshape(P, NODE_TILES * F),
        "src_t": src_t.reshape(P, GROUPS, 2 * TILES), "src_r": src_r.reshape(T_P, 2 * T_TILES),
        "dst_t": dst_t.reshape(P, GROUPS, 2 * TILES), "dst_r": dst_r.reshape(T_P, 2 * T_TILES), "dst_h": dst[:MAIN].reshape(D_ROWS, D_HALVES, HALF),
        "dst_hr": dst[MAIN:].reshape(2, 1, T_HALF),
        "e_main": e_main.reshape(GROUPS, 2 * E_ROWS, HALF), "e_ragged": e_ragged.reshape(2 * E_ROWS, T_HALF),
        "x": x, "w_dst": w1[:, F:2 * F].T, "w_src": w_src.reshape(P, P), "w_edges": w_edges.reshape(2 * E_ROWS, P), "b1": a["L0_gnn_b1"],
        "g1": a["L0_gnn_g1"], "bt1": a["L0_gnn_bt1"], "g2": a["L0_gnn_g2"], "bt2": a["L0_gnn_bt2"],
        "g3": a["L0_gnn_g3"], "bt3": a["L0_gnn_bt3"],
    }
    arrays = {k: np.ascontiguousarray(v) for k, v in arrays.items()}
    nc = bacc.Bacc("TRN2", target_bir_lowering=False, num_devices=1)
    args = [nc.dram_tensor(k, v.shape, mybir.dt.from_np(v.dtype), kind="ExternalInput").ap() for k, v in arrays.items()]
    out = nc.dram_tensor("out", (P, NODE_TILES * F), F32, kind="ExternalOutput").ap()
    build(nc, *args, out)
    r = run_bass_kernel_spmd(nc, [arrays], core_ids=[0])
    return np.asarray(r.results[0]["out"]).reshape(N_PAD, F)[:N_NODES]
```

```python
import numpy as np
import concourse.bass as bass
from concourse import mybir
from contextlib import ExitStack

F32 = mybir.dt.float32
I32 = mybir.dt.int32
ALU = mybir.AluOpType
ACT = mybir.ActivationFunctionType
AX = mybir.AxisListType

N_NODES, N_EDGES, F, EDGE_F = 12500, 200000, 64, 41
EPS = 1e-5

P = 128
HALF = 512
TILES = HALF // P
GROUPS = N_EDGES // (2 * HALF)
CHUNK = 3
CHUNKS = GROUPS // CHUNK
T_HALF = (N_EDGES - GROUPS * 2 * HALF) // 2
T_P = 80
T_TILES = T_HALF // T_P
HALVES = 2 * GROUPS + 2
MAIN = GROUPS * 2 * HALF

NODE_TILES = -(-N_NODES // P)
N_PAD = NODE_TILES * P
WIN = 84
WINDOWS = -(-N_NODES // WIN)
PAIRS = 7
BLOCKS = NODE_TILES // (2 * PAIRS)
PARTS_OF_BLOCK = [slice(0, 4), slice(4, PAIRS)]

E_ROWS = 48
D_ROWS, D_HALVES = 78, 5
EXP_CAP = 1e18
PLAIN_MAX = 40.0


class Halves:

    def __init__(self, half, tile):
        self.half, self.tile, self.tiles = half, tile, half // tile


FULL, RAGGED = Halves(HALF, P), Halves(T_HALF, T_P)


def after(eng, sem, count):
    if isinstance(count, int) and count <= 0:
        return
    eng.wait_ge(sem, count)


def rounds(eng, total, slots, body):
    for s in range(slots):
        body(s, s, 0)
    turns = total // slots
    with eng.Fori(1, turns) as i:
        for s in range(slots):
            body(i * slots + s, s, i)
    for s in range(total - turns * slots):
        body(turns * slots + s, s, turns)


class Item:

    def __init__(self, c, slot, turn):
        self.c, self.slot, self.turn = c, slot, turn
        ragged = isinstance(c, int) and c == CHUNKS
        self.size, self.groups = (RAGGED, 1) if ragged else (FULL, CHUNK)

    def cols(self, buf):
        return buf[:] if self.size is FULL else buf[:, 0, 0:self.size.half]


def pipeline(eng, slots, lag, body):
    def step(t, s, turn):
        def back(k):
            c = t - k
            if isinstance(c, int) and not 0 <= c <= CHUNKS:
                return None
            return Item(c, (s - k) % slots, turn + (s - k) // slots)
        body(back)

    turns = CHUNKS // slots
    for t in range(2 * slots):
        step(t, t % slots, t // slots)
    with eng.Fori(2, turns) as i:
        for s in range(slots):
            step(i * slots + s, s, i)
    for t in range(turns * slots, CHUNKS + 1 + lag):
        step(t, t % slots, t // slots)


def build(nc, xt, x_nodes, src_t, src_r, dst_t, dst_r, dst_h, dst_hr, e_main, e_ragged,
          x, w_dst, w_src, w_edges, b1, g1, bt1, g2, bt2, g3, bt3, out):
    ctx = ExitStack()
    with ctx:
        def dram(name, shape, dt=F32):
            return nc.dram_tensor(name, shape, dt, kind="Internal").ap()

        q_table = dram("q_table", [N_PAD, F])
        dst_f = dram("dst_f", [1, N_EDGES])
        base_f = dram("base_f", [1, HALVES])
        base_i = dram("base_i", [1, HALVES], I32)
        reach = dram("reach", [1, HALVES])
        edge_mem = dram("edge_mem", [GROUPS, P, HALF])
        edge_mem_r = dram("edge_mem_r", [P, T_HALF])

        def keep(name, shape, dt=F32):
            return ctx.enter_context(nc.sbuf_tensor(name, shape, dt))

        def sem(name):
            return ctx.enter_context(nc.semaphore(name))

        def chunk_of(c):
            return edge_mem[bass.ds(c * CHUNK, CHUNK)].rearrange("k p w -> p k w")

        ident = keep("ident", [P, P])
        fold = keep("fold", [P, P])
        base_s = keep("base_s", [1, HALVES], I32)
        base_c = keep("base_c", [1, CHUNKS + 1, 8], I32)
        base_all = keep("base_all", [P, HALVES])
        flag = keep("flag", [1, 1], I32)
        beyond = keep("beyond", [1, 1])
        flag3 = keep("flag3", [1, 1], I32)
        rel = keep("rel", [P, GROUPS, 2 * TILES])
        rel_r = keep("rel_r", [T_P, 2 * T_TILES])
        dst_tf = keep("dst_tf", [P, GROUPS, 2 * TILES])
        dst_rf = keep("dst_rf", [T_P, 2 * T_TILES])
        iota_row = keep("iota_row", [P, WIN])
        gb = keep("gb", [P, 6])
        bn1 = keep("bn1", [P, 2])
        bn2 = keep("bn2", [P, 2])
        bn3 = keep("bn3", [P, 2])
        tmp = keep("tmp", [P, 12])
        bumps = sem("bumps")

        agg = keep("agg", [P, N_PAD])
        C_SLOTS = 8
        chunks = ctx.enter_context(ExitStack())
        s_in = [chunks.enter_context(nc.sbuf_tensor(f"s_in{s}", [P, CHUNK, HALF], F32)) for s in range(C_SLOTS)]

        stage = ExitStack()
        with stage:
            def sb(name, shape, dt=F32):
                return stage.enter_context(nc.sbuf_tensor(name, shape, dt))

            S = 4
            src_idx = sb("src_idx", [P, GROUPS, 2 * TILES], I32)
            src_idx_r = sb("src_idx_r", [T_P, 2 * T_TILES], I32)
            idx = [sb(f"idx{s}", [P, 2 * TILES], I32) for s in range(S)]
            rows = [sb(f"rows{s}", [P, TILES, 2, F]) for s in range(S)]
            xg = [sb(f"xg{s}", [P, HALF]) for s in range(2)]
            e_in = [sb(f"e_in{s}", [2 * E_ROWS, HALF]) for s in range(S)]
            q_in = [sb(f"q_in{s}", [WIN, 2, F]) for s in range(S)]
            d_in = [sb(f"d_in{s}", [1, 2, HALF]) for s in range(S)]
            z_sb = [sb(f"z_sb{s}", [P, HALF]) for s in range(S)]
            hot = sb("hot", [WIN, 2, HALF])
            qw_in = sb("qw_in", [WIN, F])
            w_edge = sb("w_edge", [2 * E_ROWS, P])
            w_rows = sb("w_rows", [P, P])
            w_q = sb("w_q", [P, P])
            b1_all = sb("b1_all", [P, F])
            ones = sb("ones", [1, P])
            stats = sb("stats", [P, GROUPS + 1, 6])
            blocks = [agg[:, n * PAIRS * P:(n + 1) * PAIRS * P].rearrange("p (b w) -> p b w", b=PAIRS) for n in range(2 * BLOCKS)]
            x_in = blocks[:BLOCKS]
            q_out = blocks[BLOCKS:]
            dst_hi = sb("dst_hi", [D_ROWS, D_HALVES, HALF], I32)
            dst_hf = sb("dst_hf", [D_ROWS, D_HALVES, HALF])
            dst_ri = sb("dst_ri", [2, 1, T_HALF], I32)
            dst_rrf = sb("dst_rrf", [2, 1, T_HALF])
            low = sb("low", [D_ROWS, 3, D_HALVES])
            low_r = sb("low_r", [2, 3, 1])
            low_i = sb("low_i", [D_ROWS, D_HALVES], I32)
            low_ri = sb("low_ri", [2, 1], I32)
            reach_row = sb("reach_row", [1, HALVES])
            farthest = sb("farthest", [1, 1])
            iota_p = sb("iota_p", [P, 1])
            node_col = sb("node_col", [P, HALVES])
            win_col = sb("win_col", [P, WINDOWS])
            z_ps = [stage.enter_context(nc.psum_tensor(f"z_ps{s}", [P, HALF], F32)) for s in range(2)]
            xg_ps = [stage.enter_context(nc.psum_tensor(f"xg_ps{s}", [P, HALF], F32)) for s in range(2)]
            d_ps = stage.enter_context(nc.psum_tensor("d_ps", [P, 2, HALF], F32))
            q_ps = [stage.enter_context(nc.psum_tensor(f"q_ps{s}", [P, 4, 2 * F], F32)) for s in range(2)]
            pair = q_ps[0][:, 0, :]

            src_in, dst_in, w_in, w_in2 = sem("src_in"), sem("dst_in"), sem("w_in"), sem("w_in2")
            x_loaded = [sem(f"x_loaded{n}") for n in range(BLOCKS)]
            q_stored = sem("q_stored")
            projected, q_biased = sem("projected"), sem("q_biased")
            dst_cast, lows, bases_out, bases_in, flag_set = (sem(n) for n in ("dst_cast", "lows", "bases_out", "bases_in", "flag_set"))
            made, masks, prep = sem("made"), sem("masks"), sem("prep")
            loaded = [sem(f"loaded{s}") for s in range(S)]
            q_loaded = [sem(f"q_loaded{s}") for s in range(S)]
            gathered = [sem(f"gathered{s}") for s in range(S)]
            z_stored = [sem(f"z_stored{s}") for s in range(S)]
            idx_ready, turned, xg_ready, dst_spread, hot_ready = (
                sem(n) for n in ("idx_ready", "turned", "xg_ready", "dst_spread", "hot_ready"))
            z_ready, z_copied, z_counted = sem("z_ready"), sem("z_copied"), sem("z_counted")
            z_ahead = sem("z_ahead")
            win_loaded, win_hot, win_used = sem("win_loaded"), sem("win_hot"), sem("win_used")
            aggr, paired, rooted, bn1_steps = sem("aggr"), sem("paired"), sem("rooted"), sem("bn1_steps")
            R_SLOT, R_TURN = GROUPS % S, GROUPS // S

            blk = stage.enter_context(nc.Block())

            @blk.sync
            def _(sp):
                sp.dma_start(src_idx[:], src_t).then_inc(src_in, 16)
                sp.dma_start(dst_hi[:], dst_h).then_inc(dst_in, 16)
                sp.dma_start(dst_ri[:], dst_hr).then_inc(dst_in, 16)
                sp.dma_start(w_q[:], w_dst).then_inc(w_in, 16)
                sp.dma_start(b1_all[:], b1.partition_broadcast(P)).then_inc(w_in, 16)
                for n in range(BLOCKS):
                    sp.dma_start(x_in[n], xt[n]).then_inc(x_loaded[n], 16)
                sp.dma_start(src_idx_r[:], src_r).then_inc(w_in2, 16)
                sp.dma_start(w_rows[:], w_src).then_inc(w_in2, 16)
                sp.dma_start(w_edge[:], w_edges).then_inc(w_in2, 16)
                for n, v in enumerate((g1, bt1, g2, bt2, g3, bt3)):
                    for h in range(2):
                        sp.dma_start(gb[h * F:(h + 1) * F, n:n + 1], v.rearrange("(f a) -> f a", a=1)).then_inc(w_in2, 16)
                sp.wait_ge(dst_cast, 2)
                sp.dma_start(dst_f[:, 0:MAIN].rearrange("a (p w) -> (a p) w", p=D_ROWS),
                             dst_hf[:].rearrange("p h w -> p (h w)")).then_inc(bases_out, 16)
                sp.dma_start(dst_f[:, MAIN:].rearrange("a (p w) -> (a p) w", p=2), dst_rrf[:, 0, :]).then_inc(bases_out, 16)
                sp.wait_ge(lows, 1)
                for row, main, ragged in ((base_f, low[:, 0, :], low_r[:, 0, :]), (base_i, low_i[:], low_ri[:]),
                                          (reach, low[:, 2, :], low_r[:, 2, :])):
                    sp.dma_start(row[:, 0:2 * GROUPS].rearrange("a (p h) -> (a p) h", p=D_ROWS), main).then_inc(bases_out, 16)
                    sp.dma_start(row[:, 2 * GROUPS:].rearrange("a (p h) -> (a p) h", p=2), ragged).then_inc(bases_out, 16)
                sp.wait_ge(bases_out, 8 * 16)
                sp.dma_start(base_s[:], base_i).then_inc(bases_in, 16)
                sp.dma_start(reach_row[:], reach).then_inc(bases_in, 16)
                sp.dma_start(base_all[:], base_f.rearrange("a h -> (a h)").partition_broadcast(P)).then_inc(bases_in, 16)

                def fetch_ahead():
                    for c in range(C_SLOTS, 2 * C_SLOTS):
                        for s in range(S):
                            sp.wait_ge(z_stored[s], 16 * (-(-((c + 1) * CHUNK - s) // S)))
                        sp.dma_start(s_in[c % C_SLOTS][:], chunk_of(c)).then_inc(z_ahead, 16)

                def load(g, s, size, general):
                    if isinstance(g, int) and g == GROUPS // S * S:
                        fetch_ahead()
                    after(sp, z_ready, g - S + 1)
                    if size is FULL:
                        sp.dma_start(e_in[s][:], e_main[bass.ds(g, 1)].rearrange("a r w -> (a r) w")).then_inc(loaded[s], 16)
                    else:
                        sp.dma_start(e_in[s][:, 0:size.half], e_ragged).then_inc(loaded[s], 16)
                    sp.dma_start(d_in[s][:, :, 0:size.half],
                                 dst_f[:, bass.ds(g * 2 * HALF, 2 * size.half)].rearrange("a (h w) -> a h w", h=2)).then_inc(loaded[s], 16)
                    if not general:
                        for h in range(2):
                            base = sp.value_load(base_s[:, bass.ds(g * 2 + h, 1)], min_val=0, max_val=N_PAD - WIN)
                            sp.dma_start(q_in[s][:, h, :], q_table[bass.ds(base, WIN), :]).then_inc(q_loaded[s], 16)
                    else:
                        with sp.Fori(0, WINDOWS) as w:
                            sp.wait_ge(win_used, g * WINDOWS + w + 1)
                            sp.dma_start(qw_in[:], q_table[bass.ds(w * WIN, WIN), :]).then_inc(win_loaded, 16)

                def all_groups(general):
                    rounds(sp, GROUPS, S, lambda g, s, turn: load(g, s, FULL, general))
                    load(GROUPS, R_SLOT, RAGGED, general)
                    sp.wait_ge(z_ahead, 16 * C_SLOTS)

                sp.wait_ge(q_stored, 16 * BLOCKS)
                sp.wait_ge(flag_set, 1)
                spread = sp.value_load(flag[:], min_val=0, max_val=1)
                with sp.If(spread < 1):
                    all_groups(False)
                with sp.Else():
                    all_groups(True)
                sp.nop()

            @blk.gpsimd
            def _(gp):
                def gather(g, s, size):
                    gp.wait_ge(idx_ready, g + 1)
                    after(gp, turned, g - S + 1)
                    gp.sem_inc(bumps, 1)
                    for t in range(size.tiles):
                        for h in range(2):
                            j = h * size.tiles + t
                            gp.indirect_dma_start(out=rows[s][0:size.tile, t, h, :], out_offset=None, in_=x,
                                                  in_offset=bass.IndirectOffsetOnAxis(ap=idx[s][0:size.tile, j:j + 1], axis=0)
                                                  ).then_inc(gathered[s], 16)

                for t in (ident, fold):
                    gp.memset(t[:], 0.0).then_inc(masks, 1)
                gp.memset(ones[:], 1.0).then_inc(made, 1)
                gp.iota(iota_row[:], [[1, WIN]], base=0, channel_multiplier=0, allow_small_or_imprecise_dtypes=True).then_inc(made, 1)
                gp.iota(iota_p[:], [[0, 1]], base=0, channel_multiplier=1, allow_small_or_imprecise_dtypes=True).then_inc(made, 1)
                gp.iota(win_col[:], [[WIN, WINDOWS]], base=0, channel_multiplier=1, allow_small_or_imprecise_dtypes=True).then_inc(made, 1)
                for n, (t, off) in enumerate(((ident, 0), (fold, 0), (fold, -F), (fold, F))):
                    gp.wait_ge(masks, 2 + n)
                    gp.affine_select(out=t[:], in_=t[:], compare_op=ALU.not_equal, fill=1.0, base=off,
                                     pattern=[[-1, P]], channel_multiplier=1).then_inc(masks, 1)
                rounds(gp, GROUPS, S, lambda g, s, turn: gather(g, s, FULL))
                gather(GROUPS, R_SLOT, RAGGED)

            @blk.tensor
            def _(pe):
                pe.wait_ge(w_in, 32)
                for n in range(BLOCKS):
                    pe.wait_ge(x_loaded[n], 16)
                    for i, part in enumerate(PARTS_OF_BLOCK):
                        after(pe, q_biased, 2 * n + i - 1)
                        for b in range(part.start, part.stop):
                            mm = pe.matmul(q_ps[i][:, b - part.start, :], x_in[n][:, b, :], w_q[:], start=True, stop=True)
                        mm.then_inc(projected, 1)
                pe.wait_ge(w_in2, 15 * 16)
                pe.wait_ge(made, 4)
                pe.wait_ge(masks, 6)

                def group(g, s, turn, size, general):
                    w = size.half
                    pe.wait_ge(loaded[s], 32 * turn + 32)
                    after(pe, hot_ready, g)
                    for h in range(2):
                        mm = pe.matmul(d_ps[0:WIN, h, 0:w], ones[:, 0:WIN], d_in[s][:, h, 0:w], start=True, stop=True)
                    mm.then_inc(dst_spread, 1)
                    pe.wait_ge(gathered[s], turn * 2 * TILES * 16 + 2 * size.tiles * 16)
                    after(pe, xg_ready, g - 1)
                    for t in range(size.tiles):
                        mm = pe.transpose(xg_ps[s % 2][:, t * size.tile:(t + 1) * size.tile],
                                          rows[s][0:size.tile, t, :, :].rearrange("p h f -> p (h f)"), ident[0:size.tile, 0:size.tile])
                    mm.then_inc(turned, 1)
                    after(pe, z_copied, g - 1)
                    pe.matmul(z_ps[s % 2][:, 0:w], w_edge[:], e_in[s][:, 0:w], start=True, stop=False)

                    def windows(which, last):
                        for h in range(2):
                            mm = pe.matmul(z_ps[s % 2][h * F:(h + 1) * F, 0:w], which(h), hot[:, h, 0:w], start=False, stop=last)
                        return mm

                    pe.wait_ge(xg_ready, g + 1)
                    if not general:
                        pe.matmul(z_ps[s % 2][:, 0:w], w_rows[:], xg[s % 2][:, 0:w], start=False, stop=False)
                        pe.wait_ge(q_loaded[s], 32 * turn + 32)
                        pe.wait_ge(hot_ready, g + 1)
                        windows(lambda h: q_in[s][:, h, :], True).then_inc(z_ready, 1)
                    else:
                        pe.sem_inc(bumps, 1)
                        with pe.Fori(0, WINDOWS) as k:
                            pe.wait_ge(win_loaded, (g * WINDOWS + k + 1) * 16)
                            pe.wait_ge(win_hot, g * WINDOWS + k + 1)
                            windows(lambda h: qw_in[:], False).then_inc(win_used, 1)
                        pe.matmul(z_ps[s % 2][:, 0:w], w_rows[:], xg[s % 2][:, 0:w], start=False, stop=True).then_inc(z_ready, 1)

                def all_groups(general):
                    rounds(pe, GROUPS, S, lambda g, s, turn: group(g, s, turn, FULL, general))
                    group(GROUPS, R_SLOT, R_TURN, RAGGED, general)

                pe.wait_ge(flag_set, 1)
                spread = pe.value_load(flag[:], min_val=0, max_val=1)
                with pe.If(spread < 1):
                    all_groups(False)
                with pe.Else():
                    pe.sem_inc(win_used, 1)
                    all_groups(True)
                pair_sums(pe, fold, tmp, pair, aggr, paired)

            @blk.scalar
            def _(act):
                q_view = q_table.rearrange("(p n b) f -> n p (b f)", p=P, b=2 * PAIRS)
                for n in range(BLOCKS):
                    act.wait_ge(q_biased, 2 * n + 2)
                    act.dma_start(q_view[n], q_out[n].rearrange("p b f -> p (b f)")).then_inc(q_stored, 16)

                def copy_rows(g, s, size):
                    act.wait_ge(turned, g + 1)
                    after(act, z_ready, g - 1)
                    act.activation(xg[s % 2][:, 0:size.half], xg_ps[s % 2][:, 0:size.half], ACT.Copy).then_inc(xg_ready, 1)

                def copy_z(g, s, turn, size):
                    act.wait_ge(z_ready, g + 1)
                    after(act, z_counted, g - S + 1)
                    after(act, z_stored[s], 16 * turn)
                    act.activation(z_sb[s][:, 0:size.half], z_ps[s % 2][:, 0:size.half], ACT.Copy).then_inc(z_copied, 1)
                    act.wait_ge(z_copied, g + 1)
                    to = edge_mem[bass.ds(g, 1)].rearrange("a p w -> (a p) w") if size is FULL else edge_mem_r
                    act.dma_start(to, z_sb[s][:, 0:size.half]).then_inc(z_stored[s], 16)

                def both(g, s, turn, size):
                    copy_rows(g, s, size)
                    copy_z(g, s, turn, size)
                rounds(act, GROUPS, S, lambda g, s, turn: both(g, s, turn, FULL))
                both(GROUPS, R_SLOT, R_TURN, RAGGED)
                for s in range(S):
                    act.wait_ge(z_stored[s], 16 * (GROUPS // S + (s <= R_SLOT)))
                act.wait_ge(aggr, 3)
                act.activation(tmp[:, 7:8], tmp[:, 6:7], ACT.Sqrt).then_inc(rooted, 1)

            @blk.vector
            def _(v):
                def indices(g, s):
                    v.tensor_copy(idx[s][:], src_idx[:, bass.ds(g, 1), :].rearrange("p a j -> p (a j)")).then_inc(idx_ready, 1)

                v.wait_ge(src_in, 16)
                for s in range(S):
                    indices(s, s)
                v.wait_ge(dst_in, 32)
                v.tensor_copy(dst_hf[:], dst_hi[:]).then_inc(dst_cast, 1)
                v.tensor_copy(dst_rrf[:], dst_ri[:]).then_inc(dst_cast, 1)
                v.wait_ge(dst_cast, 2)
                for wide, lo in ((dst_hf, low), (dst_rrf, low_r)):
                    v.tensor_reduce(lo[:, 0, :], wide[:], AX.X, ALU.min).then_inc(prep, 1)
                    v.tensor_reduce(lo[:, 1, :], wide[:], AX.X, ALU.max).then_inc(prep, 1)
                v.wait_ge(prep, 4)
                for lo in (low, low_r):
                    v.tensor_scalar(lo[:, 0, :], lo[:, 0, :], float(N_PAD - WIN), None, ALU.min).then_inc(prep, 1)
                v.wait_ge(prep, 6)
                for lo, lo_i in ((low, low_i), (low_r, low_ri)):
                    v.tensor_copy(lo_i[:], lo[:, 0, :]).then_inc(prep, 1)
                    v.tensor_tensor(lo[:, 2, :], lo[:, 1, :], lo[:, 0, :], ALU.subtract).then_inc(prep, 1)
                v.wait_ge(prep, 10)
                v.sem_inc(lows, 1)

                for n in range(BLOCKS):
                    for i, part in enumerate(PARTS_OF_BLOCK):
                        pairs = part.stop - part.start
                        v.wait_ge(projected, 2 * n + i + 1)
                        v.tensor_tensor(q_out[n][:, part, :].rearrange("p b (h f) -> p (b h) f", f=F),
                                        q_ps[i][:, 0:pairs, :].rearrange("p b (h f) -> p (b h) f", f=F),
                                        b1_all[:].rearrange("p (a f) -> p a f", a=1).broadcast_to([P, 2 * pairs, F]), ALU.add).then_inc(q_biased, 1)

                v.wait_ge(bases_in, 48)
                v.wait_ge(made, 4)
                v.tensor_reduce(farthest[:], reach_row[:], AX.X, ALU.max).then_inc(prep, 1)
                v.tensor_scalar(node_col[:], base_all[:], iota_p[:], None, ALU.add).then_inc(prep, 1)
                v.wait_ge(prep, 12)
                v.tensor_scalar(beyond[:], farthest[:], float(WIN), None, ALU.is_ge).then_inc(prep, 1)
                v.wait_ge(prep, 13)
                v.tensor_copy(flag[:], beyond[:]).then_inc(flag_set, 1)

                def group(g, s, size, general, more):
                    v.wait_ge(dst_spread, g + 1)
                    after(v, z_ready, g)
                    if not general:
                        for h in range(2):
                            hots = v.tensor_scalar(hot[:, h, 0:size.half], d_ps[0:WIN, h, 0:size.half],
                                                   node_col[0:WIN, bass.ds(g * 2 + h, 1)], None, ALU.is_equal)
                        hots.then_inc(hot_ready, 1)
                    else:
                        v.sem_inc(bumps, 1)
                        with v.Fori(0, WINDOWS) as k:
                            v.wait_ge(win_used, g * WINDOWS + k + 1)
                            for h in range(2):
                                hots = v.tensor_scalar(hot[:, h, 0:size.half], d_ps[0:WIN, h, 0:size.half],
                                                       win_col[0:WIN, bass.ds(k, 1)], None, ALU.is_equal)
                            hots.then_inc(win_hot, 1)
                        v.wait_ge(win_hot, g * WINDOWS + WINDOWS)
                        v.sem_inc(hot_ready, 1)
                    if more:
                        v.wait_ge(turned, g + 1)
                        indices(g + S, s)
                    v.wait_ge(z_copied, g + 1)
                    v.bn_stats(stats[:, bass.ds(g, 1), :].rearrange("p a k -> p (a k)"), z_sb[s][:, 0:size.half]).then_inc(z_counted, 1)

                def all_groups(general):
                    for g in range(S):
                        group(g, g, FULL, general, True)
                    with v.Fori(1, GROUPS // S - 1) as i:
                        for s in range(S):
                            group(i * S + s, s, FULL, general, True)
                    for g in range(S * (GROUPS // S - 1), GROUPS):
                        group(g, g % S, FULL, general, g + S < GROUPS)
                        if g + S == GROUPS:
                            v.tensor_copy(idx[g % S][0:T_P, 0:2 * T_TILES], src_idx_r[:]).then_inc(idx_ready, 1)
                    group(GROUPS, R_SLOT, RAGGED, general, False)

                v.wait_ge(flag_set, 1)
                v.wait_ge(w_in2, 15 * 16)
                spread = v.value_load(flag[:], min_val=0, max_val=1)
                with v.If(spread < 1):
                    all_groups(False)
                with v.Else():
                    all_groups(True)
                norm_coefficients(v, stats[:], z_counted, GROUPS + 1, gb[:, 0:1], gb[:, 1:2], bn1,
                                  tmp, pair, aggr, paired, rooted, bn1_steps)


        stage = ExitStack()
        with stage:
            def sb(name, shape, dt=F32):
                return stage.enter_context(nc.sbuf_tensor(name, shape, dt))

            s_buf_r = sb("s_buf_r", [P, T_HALF])
            S = C_SLOTS
            stats = sb("stats2", [P, GROUPS + 1, 6])
            dst_ti = sb("dst_ti", [P, GROUPS, 2 * TILES], I32)
            dst_tri = sb("dst_tri", [T_P, 2 * T_TILES], I32)
            pair_ps = stage.enter_context(nc.psum_tensor("pair_ps", [P, 512], F32))
            z_loaded = [sem(f"z_loaded{s}") for s in range(S)]
            r_loaded, gated, s_counted = sem("r_loaded"), sem("gated"), sem("s_counted")
            tiles_in, tiles_cast = sem("tiles_in"), sem("tiles_cast")
            aggr, paired, rooted, bn2_steps = sem("aggr2"), sem("paired2"), sem("rooted2"), sem("bn2_steps")
            high = sb("high", [P, 2])
            high_count = sb("high_count", [1, 1])
            ones_col = sb("ones_col", [P, 1])
            ones_set, high_steps, high_set, highs = (sem(n) for n in ("ones_set", "high_steps", "high_set", "highs"))

            def in_order(eng, body):
                rounds(eng, CHUNKS - S, S, lambda n, s, turn: body(n, n + S, s, turn))
                for c in range(S):
                    body(CHUNKS - S + c, c, c, -(-(CHUNKS - S - c) // S))

            def last_in_slot(n, c):
                if isinstance(c, int) and c < S:
                    return (CHUNKS - S - c - 1) // S * S + c
                return n - S

            blk = stage.enter_context(nc.Block())

            @blk.sync
            def _(sp):
                def load(n, c, s, turn):
                    if isinstance(n, int) and n < S:
                        return
                    after(sp, s_counted, last_in_slot(n, c) + 1)
                    sp.dma_start(s_in[s][:], chunk_of(c)).then_inc(z_loaded[s], 16)
                in_order(sp, load)
                sp.dma_start(s_buf_r[:], edge_mem_r).then_inc(r_loaded, 16)
                sp.dma_start(dst_ti[:], dst_t).then_inc(tiles_in, 16)
                sp.dma_start(dst_tri[:], dst_r).then_inc(tiles_in, 16)

            @blk.scalar
            def _(act):
                def gate(n, c, s, turn):
                    after(act, z_loaded[s], 16 * turn)
                    act.activation(s_in[s][:], s_in[s][:], ACT.Sigmoid, scale=bn1[:, 0:1], bias=bn1[:, 1:2]).then_inc(gated, 1)
                in_order(act, gate)
                act.wait_ge(r_loaded, 16)
                act.activation(s_buf_r[:], s_buf_r[:], ACT.Sigmoid, scale=bn1[:, 0:1], bias=bn1[:, 1:2]).then_inc(gated, 1)
                act.wait_ge(aggr, 3)
                act.activation(tmp[:, 7:8], tmp[:, 6:7], ACT.Sqrt).then_inc(rooted, 1)

            @blk.gpsimd
            def _(gp):
                gp.memset(ones_col[:], 1.0).then_inc(ones_set, 1)
                gp.memset(agg[:], 0.0)

            @blk.vector
            def _(v):
                def count(n, c, s, turn):
                    v.wait_ge(gated, n + 1)
                    for k in range(CHUNK):
                        ins = v.bn_stats(stats[:, bass.ds(c * CHUNK + k, 1), :].rearrange("p a k -> p (a k)"), s_in[s][:, k, :])
                    ins.then_inc(s_counted, 1)
                in_order(v, count)
                v.wait_ge(gated, CHUNKS + 1)
                v.bn_stats(stats[:, GROUPS, :], s_buf_r[:]).then_inc(s_counted, 1)
                norm_coefficients(v, stats[:], s_counted, CHUNKS + 1, gb[:, 2:3], gb[:, 3:4], bn2,
                                  tmp, pair_ps, aggr, paired, rooted, bn2_steps)
                v.tensor_tensor(high[:, 0:1], bn2[:, 0:1], bn2[:, 1:2], ALU.add).then_inc(high_steps, 1)
                v.wait_ge(high_steps, 1)
                v.tensor_tensor(high[:, 0:1], high[:, 0:1], bn2[:, 1:2], ALU.max).then_inc(high_steps, 1)
                v.wait_ge(high_steps, 2)
                v.tensor_scalar(high[:, 1:2], high[:, 0:1], PLAIN_MAX, None, ALU.is_ge).then_inc(high_set, 1)
                v.wait_ge(highs, 1)
                v.tensor_tensor(high_count[:], pair_ps[0:1, 2:3], beyond[:], ALU.add).then_inc(high_steps, 1)
                v.wait_ge(high_steps, 3)
                v.tensor_scalar(high_count[:], high_count[:], 0.5, None, ALU.is_ge).then_inc(high_steps, 1)
                v.wait_ge(high_steps, 4)
                v.tensor_copy(flag3[:], high_count[:])
                v.wait_ge(tiles_in, 32)
                v.tensor_copy(base_c[:, 0:CHUNKS, 0:2 * CHUNK], base_s[:, 0:2 * GROUPS].rearrange("a (c j) -> a c j", c=CHUNKS))
                v.tensor_copy(base_c[:, CHUNKS, 0:2], base_s[:, 2 * GROUPS:])
                v.tensor_copy(dst_tf[:], dst_ti[:]).then_inc(tiles_cast, 1)
                v.tensor_copy(dst_rf[:], dst_tri[:]).then_inc(tiles_cast, 1)
                v.wait_ge(tiles_cast, 2)
                v.tensor_tensor(rel[:].rearrange("p g (h t) -> p g h t", h=2), dst_tf[:].rearrange("p g (h t) -> p g h t", h=2),
                                base_all[:, 0:2 * GROUPS].rearrange("p (g h a) -> p g h a", h=2, a=1).broadcast_to([P, GROUPS, 2, TILES]), ALU.subtract)
                v.tensor_tensor(rel_r[:].rearrange("p (h t) -> p h t", h=2), dst_rf[:].rearrange("p (h t) -> p h t", h=2),
                                base_all[0:T_P, 2 * GROUPS:].rearrange("p (h a) -> p h a", a=1).broadcast_to([T_P, 2, T_TILES]), ALU.subtract)

            @blk.tensor
            def _(pe):
                pair_sums(pe, fold, tmp, pair_ps, aggr, paired)
                pe.wait_ge(ones_set, 1)
                pe.wait_ge(high_set, 1)
                pe.matmul(pair_ps[0:1, 2:3], high[:, 1:2], ones_col[:], start=True, stop=True).then_inc(highs, 1)

        stage = ExitStack()
        with stage:
            def sb(name, shape, dt=F32):
                return stage.enter_context(nc.sbuf_tensor(name, shape, dt))

            H, BATCH = 4, 4
            h_buf = [sb(f"h_buf{s}", [P, CHUNK, HALF]) for s in range(H)]
            lin = [sb(f"lin{s}", [P, CHUNK, HALF]) for s in range(2)]
            h_rows = [sb(f"h_rows{s}", [P, CHUNK, TILES, P]) for s in range(2)]
            near = [sb(f"near{s}", [P, CHUNK * 2 * TILES, WIN]) for s in range(2)]
            win_start = sb("win_start", [P, WINDOWS])
            win_rel = sb("win_rel", [P, 2 * TILES])
            turn_ps = [stage.enter_context(nc.psum_tensor(f"turn_ps{s}", [P, CHUNK, TILES, P], F32)) for s in range(2)]
            sum_ps = [stage.enter_context(nc.psum_tensor(f"sum_ps{s}", [P, 512], F32)) for s in range(2)]

            z_loaded = [sem(f"z_loaded3{s}") for s in range(S)]
            gated = sem("gated3")
            cleared, raised, capped, logged, lined, maxed, h_ready = (
                sem(n) for n in ("cleared", "raised", "capped", "logged", "lined", "maxed", "h_ready"))
            h_turned, rows_ready, near_ready, summed, rel_made, win_near, win_summed, win_added = (
                sem(n) for n in ("h_turned", "rows_ready", "near_ready", "summed", "rel_made", "win_near", "win_summed", "win_added"))

            def here(m):
                return isinstance(m.c, int) and m.c < S

            blk = stage.enter_context(nc.Block())

            @blk.sync
            def _(sp):
                def step(back):
                    m = back(0)
                    if m and not here(m):
                        after(sp, h_ready, m.c - S + 1)
                        sp.dma_start(m.cols(s_in[m.slot]), chunk_of(m.c) if m.size is FULL else edge_mem_r).then_inc(z_loaded[m.slot], 16)
                pipeline(sp, S, 0, step)

            def by_path(eng, lag, step):
                rare = eng.value_load(flag3[:], min_val=0, max_val=1)
                with eng.If(rare < 1):
                    pipeline(eng, S, lag, lambda back: step(back, False))
                with eng.Else():
                    pipeline(eng, S, lag, lambda back: step(back, True))
                eng.nop()

            @blk.scalar
            def _(act):
                def gate(m):
                    act.wait_ge(z_loaded[m.slot], 16 * m.turn)
                    act.activation(m.cols(s_in[m.slot]), m.cols(s_in[m.slot]), ACT.Sigmoid, scale=bn1[:, 0:1], bias=bn1[:, 1:2]).then_inc(gated, 1)

                act.preload_act_table_set("natural_log_exp_and_others")

                def step(back, general):
                    if m := back(1):
                        act.wait_ge(capped if general else raised, m.c + 1)
                        act.activation(m.cols(h_buf[m.slot % H]), m.cols(h_buf[m.slot % H]), ACT.Ln, bias=1.0).then_inc(logged, 1)
                    if (m := back(0)) and m.slot % BATCH == 0 and not here(m):
                        act.preload_act_table_set("sigmoid_and_others")
                        for k in range(BATCH):
                            if ahead := back(-k):
                                gate(ahead)
                        act.preload_act_table_set("natural_log_exp_and_others")
                    if m := back(0):
                        if not here(m):
                            act.wait_ge(gated, m.c - S + 1)
                        after(act, h_turned, m.c - H + 1)
                        act.activation(m.cols(h_buf[m.slot % H]), m.cols(s_in[m.slot]), ACT.Exp, scale=bn2[:, 0:1], bias=bn2[:, 1:2]).then_inc(raised, 1)
                        if general:
                            after(act, maxed, m.c - 1)
                            act.activation(m.cols(lin[m.slot % 2]), m.cols(s_in[m.slot]), ACT.Identity,
                                           scale=bn2[:, 0:1], bias=bn2[:, 1:2]).then_inc(lined, 1)
                by_path(act, 1, step)

            @blk.gpsimd
            def _(gp):
                gp.iota(win_start[:], [[WIN, WINDOWS]], base=0, channel_multiplier=0, allow_small_or_imprecise_dtypes=True).then_inc(cleared, 1)

                def step(back, general):
                    if m := back(1):
                        gp.wait_ge(maxed if general else logged, m.c + 1)
                        gp.tensor_tensor(m.cols(h_buf[m.slot % H]), m.cols(h_buf[m.slot % H]), m.cols(s_in[m.slot]), ALU.mult).then_inc(h_ready, 1)
                by_path(gp, 1, step)

            @blk.tensor
            def _(pe):
                def window_sums(m, k):
                    n = m.size
                    for h in range(2):
                        for t in range(n.tiles):
                            mm = pe.matmul(sum_ps[m.slot % 2][h * F:(h + 1) * F, k * WIN:(k + 1) * WIN], h_rows[m.slot % 2][0:n.tile, k, t, h * F:(h + 1) * F],
                                           near[m.slot % 2][0:n.tile, (2 * k + h) * n.tiles + t, :], start=(t == 0), stop=(t == n.tiles - 1))
                    return mm

                def step(back, general):
                    if m := back(2):
                        pe.wait_ge(h_ready, m.c + 1)
                        after(pe, rows_ready, m.c - 1)
                        for k in range(m.groups):
                            for t in range(m.size.tiles):
                                mm = pe.transpose(turn_ps[m.slot % 2][0:m.size.tile, k, t, :], h_buf[m.slot % H][:, k, t * m.size.tile:(t + 1) * m.size.tile], ident[:])
                        mm.then_inc(h_turned, 1)
                    if m := back(3):
                        pe.wait_ge(rows_ready, m.c + 1)
                        for k in range(m.groups):
                            g = m.c * CHUNK + k
                            if not general:
                                pe.wait_ge(near_ready, g + 1)
                                if k == 0:
                                    after(pe, win_added, (m.c - 1) * CHUNK)
                                window_sums(m, k).then_inc(summed, 1)
                            else:
                                pe.sem_inc(bumps, 1)
                                with pe.Fori(0, WINDOWS) as w:
                                    pe.wait_ge(win_near, g * WINDOWS + w + 1)
                                    window_sums(m, k).then_inc(win_summed, 1)
                                pe.wait_ge(win_summed, (g + 1) * WINDOWS)
                                pe.sem_inc(summed, 1)
                by_path(pe, 3, step)

            @blk.vector
            def _(v):
                def equal(hots, places):
                    shape = list(hots.shape)
                    return v.tensor_tensor(hots, iota_row[0:shape[0], :].rearrange("p (a n) -> p a n", a=1).broadcast_to(shape),
                                           places.rearrange("p (j a) -> p j a", a=1).broadcast_to(shape), ALU.is_equal)

                def hots_of(m, k):
                    n = 2 * m.size.tiles
                    return near[m.slot % 2][0:m.size.tile, k * n:(k + 1) * n, :]

                def dst_of(m, table, table_r, k):
                    if m.size is RAGGED:
                        return table_r[:]
                    return table[:, bass.ds(m.c * CHUNK + k, 1), :].rearrange("p g j -> p (g j)")

                def add(m, k, h, base):
                    lanes = agg[h * F:(h + 1) * F, bass.ds(base, WIN)]
                    return v.tensor_tensor(lanes, lanes, sum_ps[m.slot % 2][h * F:(h + 1) * F, k * WIN:(k + 1) * WIN], ALU.add)

                def copy_rows(m):
                    if m:
                        v.wait_ge(h_turned, m.c + 1)
                        after(v, summed, (m.c - 1) * CHUNK)
                        at = (slice(0, m.size.tile), slice(0, m.groups), slice(0, m.size.tiles))
                        v.tensor_copy(h_rows[m.slot % 2][at], turn_ps[m.slot % 2][at]).then_inc(rows_ready, 1)

                def step_plain(back):
                    sums, hots = back(4), back(2)
                    if m := hots:
                        after(v, summed, (m.c - 1) * CHUNK)
                    for k in range(CHUNK):
                        if (m := hots) and k < m.groups:
                            equal(hots_of(m, k), dst_of(m, rel, rel_r, k)).then_inc(near_ready, 1)
                        if (m := sums) and k == 0:
                            row = base_c[:, bass.ds(m.c, 1), 0:2 * m.groups].rearrange("a c j -> a (c j)")
                            _, bases = nc.values_load_multi_w_load_instructions(
                                row, engines=[mybir.EngineType.DVE], min_val=0, max_val=N_PAD - WIN)
                        if (m := sums) and k < m.groups:
                            g = m.c * CHUNK + k
                            if k == 0:
                                v.wait_ge(summed, (m.c * CHUNK) + m.groups)
                            after(v, win_added, g)
                            add(m, k, 0, bases[2 * k])
                            add(m, k, 1, bases[2 * k + 1]).then_inc(win_added, 1)
                    copy_rows(back(2))

                def step_general(back):
                    if m := back(1):
                        v.wait_ge(logged, m.c + 1)
                        v.wait_ge(lined, m.c + 1)
                        v.tensor_tensor(m.cols(h_buf[m.slot % H]), m.cols(h_buf[m.slot % H]), m.cols(lin[m.slot % 2]), ALU.max).then_inc(maxed, 1)
                    copy_rows(back(2))
                    if m := back(3):
                        part = win_rel[0:m.size.tile, 0:2 * m.size.tiles]
                        for k in range(m.groups):
                            g = m.c * CHUNK + k
                            with v.Fori(0, WINDOWS) as w:
                                v.wait_ge(win_added, g * WINDOWS + w + 1)
                                v.tensor_scalar(part, dst_of(m, dst_tf, dst_rf, k), win_start[0:m.size.tile, bass.ds(w, 1)],
                                                None, ALU.subtract).then_inc(rel_made, 1)
                                v.wait_ge(rel_made, g * WINDOWS + w + 1)
                                equal(hots_of(m, k), part).then_inc(win_near, 1)
                                v.wait_ge(win_summed, g * WINDOWS + w + 1)
                                add(m, k, 0, w * WIN)
                                add(m, k, 1, w * WIN).then_inc(win_added, 1)
                    if m := back(0):
                        v.wait_ge(raised, m.c + 1)
                        v.tensor_scalar(m.cols(h_buf[m.slot % H]), m.cols(h_buf[m.slot % H]), EXP_CAP, None, ALU.min).then_inc(capped, 1)

                v.wait_ge(cleared, 1)
                rare = v.value_load(flag3[:], min_val=0, max_val=1)
                with v.If(rare < 1):
                    pipeline(v, S, 4, step_plain)
                with v.Else():
                    v.sem_inc(win_added, 1)
                    pipeline(v, S, 4, step_general)
                v.nop()

        chunks.close()
        stage = ExitStack()
        with stage:
            def sb(name, shape, dt=F32):
                return stage.enter_context(nc.sbuf_tensor(name, shape, dt))

            S, V = 4, 3
            N_HALF = N_NODES // 2
            COLS = 500
            PARTS = [slice(c, min(c + COLS, N_HALF)) for c in range(0, N_HALF, COLS)]
            N = len(PARTS)
            x_sb = sb("x_sb", [P, N_HALF])
            total = sb("total", [P, N_HALF])
            square = [sb(f"square{s}", [P, COLS]) for s in range(S)]
            inv_dev = [sb(f"inv_dev{s}", [P, COLS]) for s in range(S)]
            refine = [sb(f"refine{s}", [P, COLS]) for s in range(V)]
            eps = sb("eps", [P, 1])
            y = sb("y", [P, N_HALF])
            average = sb("average", [P, P])
            centre = sb("centre", [P, P])
            centre_x = sb("centre_x", [P, P])
            centre_t = sb("centre_t", [P, P])
            stats = sb("stats3", [P, N, 6])
            shift = sb("shift", [P, 1])
            y_ps = [stage.enter_context(nc.psum_tensor(f"y_ps{s}", [P, 512], F32)) for s in range(S)]
            var_ps = [stage.enter_context(nc.psum_tensor(f"var_ps{s}", [P, 512], F32)) for s in range(V)]
            pair_ps = stage.enter_context(nc.psum_tensor("pair_ps4", [P, 512], F32))

            x_in4, folded, f_copied, f_counted, aggr, paired, rooted, bn3_steps = (
                sem(n) for n in ("x_in4", "folded", "f_copied", "f_counted", "aggr3", "paired3", "rooted3", "bn3_steps"))
            averages, centres, scaled, shift_summed, shift_set = (
                sem(n) for n in ("averages", "centres", "scaled", "shift_summed", "shift_set"))
            centred, squared, averaged, logged, inverted, inv_squared, multiplied, divided, refined, normed, stored = (
                sem(n) for n in ("centred", "squared", "averaged", "logged3", "inverted", "inv_squared", "multiplied",
                                 "divided", "refined", "normed", "stored"))

            def width(n):
                return PARTS[n].stop - PARTS[n].start

            blk = stage.enter_context(nc.Block())

            @blk.sync
            def _(sp):
                sp.dma_start(x_sb[:], x_nodes).then_inc(x_in4, 16)
                for n in range(N):
                    sp.wait_ge(normed, n + 1)
                    sp.dma_start(out[:, PARTS[n]], y[:, PARTS[n]]).then_inc(stored, 16)
                sp.wait_ge(stored, 16 * N)

            @blk.gpsimd
            def _(gp):
                gp.memset(eps[:], EPS).then_inc(averages, 1)
                gp.memset(average[:], 0.0).then_inc(averages, 1)
                gp.wait_ge(averages, 2)
                for h in range(2):
                    lanes = slice(h * F, (h + 1) * F)
                    gp.memset(average[lanes, lanes], 1.0 / F).then_inc(averages, 1)
                gp.wait_ge(averages, 4)
                gp.tensor_tensor(centre[:], ident[:], average[:], ALU.subtract).then_inc(centres, 1)
                gp.wait_ge(centres, 1)
                gp.tensor_tensor(centre_x[:], centre[:], centre[:], ALU.add).then_inc(centres, 1)

                def finish(n):
                    gp.wait_ge(divided, n + 1)
                    gp.wait_ge(refined, n + 1)
                    gp.tensor_tensor(y[:, PARTS[n]], y[:, PARTS[n]], refine[n % V][:, 0:width(n)], ALU.mult).then_inc(normed, 1)

                for n in range(N):
                    part = inv_dev[n % S][:, 0:width(n)]
                    gp.wait_ge(inverted, n + 1)
                    after(gp, normed, n - V + 1)
                    gp.tensor_tensor(refine[n % V][:, 0:width(n)], part, part, ALU.mult).then_inc(inv_squared, 1)
                    if n > 0:
                        finish(n - 1)
                finish(N - 1)

            @blk.tensor
            def _(pe):
                for n in range(N):
                    after(pe, f_counted, n - S + 1)
                    after(pe, f_copied, n - S + 1)
                    for h in range(2):
                        mm = pe.matmul(y_ps[n % S][h * F:(h + 1) * F, 0:width(n)], fold[:, 0:F],
                                       agg[:, h * N_HALF + PARTS[n].start:h * N_HALF + PARTS[n].stop], start=True, stop=True)
                    mm.then_inc(folded, 1)
                pair_sums(pe, fold, tmp, pair_ps, aggr, paired)
                pe.wait_ge(x_in4, 16)
                pe.wait_ge(f_copied, N)
                pe.wait_ge(averages, 4)
                pe.wait_ge(centres, 2)
                pe.wait_ge(scaled, 1)
                pe.matmul(pair_ps[:, 2:3], centre[:], bn3[:, 1:2], start=True, stop=True).then_inc(shift_summed, 1)

                def variance(n):
                    pe.wait_ge(squared, n + 1)
                    after(pe, multiplied, n - V + 1)
                    pe.matmul(var_ps[n % V][:, 0:width(n)], average[:], square[n % S][:, 0:width(n)], start=True, stop=True).then_inc(averaged, 1)

                for n in range(N):
                    after(pe, divided, n - S + 1)
                    pe.matmul(y_ps[n % S][:, 0:width(n)], centre_x[:], x_sb[:, PARTS[n]], start=True, stop=False)
                    pe.matmul(y_ps[n % S][:, 0:width(n)], centre_t[:], total[:, PARTS[n]], start=False, stop=True).then_inc(centred, 1)
                    if n > 0:
                        variance(n - 1)
                variance(N - 1)

            @blk.scalar
            def _(act):
                for n in range(N):
                    act.wait_ge(folded, n + 1)
                    act.wait_ge(f_counted, n + 1)
                    act.activation(total[:, PARTS[n]], y_ps[n % S][:, 0:width(n)], ACT.Copy).then_inc(f_copied, 1)
                act.wait_ge(aggr, 3)
                act.activation(tmp[:, 7:8], tmp[:, 6:7], ACT.Sqrt).then_inc(rooted, 1)
                act.preload_act_table_set("natural_log_exp_and_others")
                act.wait_ge(averages, 4)
                act.wait_ge(shift_set, 1)

                def invert(n):
                    part = inv_dev[n % S][:, 0:width(n)]
                    act.wait_ge(averaged, n + 1)
                    after(act, divided, n - S + 1)
                    act.activation(part, var_ps[n % V][:, 0:width(n)], ACT.Ln, bias=eps[:]).then_inc(logged, 1)
                    act.wait_ge(logged, n + 1)
                    act.activation(part, part, ACT.Exp, scale=-0.5).then_inc(inverted, 1)

                for n in range(N):
                    act.wait_ge(centred, n + 1)
                    after(act, averaged, n - S + 1)
                    act.activation(square[n % S][:, 0:width(n)], y_ps[n % S][:, 0:width(n)], ACT.Square, bias=shift[:]).then_inc(squared, 1)
                    if n > 0:
                        invert(n - 1)
                invert(N - 1)

            @blk.vector
            def _(v):
                for n in range(N):
                    v.wait_ge(folded, n + 1)
                    v.bn_stats(stats[:, n, :], y_ps[n % S][:, 0:width(n)]).then_inc(f_counted, 1)
                norm_coefficients(v, stats[:], f_counted, N, gb[:, 4:5], gb[:, 5:6], bn3,
                                  tmp, pair_ps, aggr, paired, rooted, bn3_steps)
                v.wait_ge(centres, 1)
                v.tensor_scalar(centre_t[:], centre[:], bn3[:, 0:1], None, ALU.mult).then_inc(scaled, 1)
                v.wait_ge(shift_summed, 1)
                v.tensor_copy(shift[:], pair_ps[:, 2:3]).then_inc(shift_set, 1)
                v.wait_ge(shift_set, 1)
                for n in range(N):
                    part = refine[n % V][:, 0:width(n)]
                    v.wait_ge(inv_squared, n + 1)
                    v.scalar_tensor_tensor(part, var_ps[n % V][:, 0:width(n)], eps[:], part, ALU.add, ALU.mult).then_inc(multiplied, 1)
                    v.scalar_tensor_tensor(y[:, PARTS[n]], y_ps[n % S][:, 0:width(n)], shift[:], inv_dev[n % S][:, 0:width(n)],
                                           ALU.add, ALU.mult).then_inc(divided, 1)
                    v.wait_ge(multiplied, n + 1)
                    v.tensor_scalar(part, part, -0.5, 1.5, ALU.mult, ALU.add).then_inc(refined, 1)


def pair_sums(pe, fold, tmp, pair, aggr, paired):
    pe.wait_ge(aggr, 1)
    pe.matmul(pair[:, 0:1], fold[:], tmp[:, 0:1], start=True, stop=True).then_inc(paired, 1)
    pe.wait_ge(aggr, 2)
    pe.matmul(pair[:, 1:2], fold[:], tmp[:, 4:5], start=True, stop=True).then_inc(paired, 1)


def norm_coefficients(v, stats, counted, count, gamma, beta, coef, tmp, pair, aggr, paired, rooted, steps):
    n = [0]

    def step(ins):
        n[0] += 1
        ins.then_inc(steps, 1)
        v.wait_ge(steps, n[0])

    v.wait_ge(counted, count)
    step(v.bn_aggr(tmp[:, 0:2], stats))
    v.sem_inc(aggr, 1)
    v.wait_ge(paired, 1)
    step(v.tensor_scalar(tmp[:, 2:3], pair[:, 0:1], 0.5, None, ALU.mult))
    step(v.tensor_tensor(tmp[:, 3:4], tmp[:, 0:1], tmp[:, 2:3], ALU.subtract))
    step(v.tensor_tensor(tmp[:, 3:4], tmp[:, 3:4], tmp[:, 3:4], ALU.mult))
    step(v.tensor_tensor(tmp[:, 4:5], tmp[:, 1:2], tmp[:, 3:4], ALU.add))
    v.sem_inc(aggr, 1)
    v.wait_ge(paired, 2)
    step(v.tensor_scalar(tmp[:, 6:7], pair[:, 1:2], 0.5, EPS, ALU.mult, ALU.add))
    v.sem_inc(aggr, 1)
    v.wait_ge(rooted, 1)
    step(v.reciprocal(tmp[:, 8:9], tmp[:, 7:8]))
    step(v.tensor_tensor(coef[:, 0:1], tmp[:, 8:9], gamma, ALU.mult))
    step(v.tensor_tensor(tmp[:, 9:10], tmp[:, 2:3], coef[:, 0:1], ALU.mult))
    step(v.tensor_tensor(coef[:, 1:2], beta, tmp[:, 9:10], ALU.subtract))


def kernel(**inputs):
    import concourse.bacc as bacc
    from concourse.bass_utils import run_bass_kernel_spmd

    a = {k: np.asarray(v) for k, v in inputs.items()}
    x, src, dst, e = a["x"], a["src"], a["dst"], a["edge_attr_41"]
    w1 = a["L0_gnn_W1"]
    x_pad = np.zeros((N_PAD, F), x.dtype)
    x_pad[:N_NODES] = x
    xt = x_pad.reshape(P, BLOCKS, PAIRS, 2, F).transpose(1, 3, 4, 2, 0).reshape(BLOCKS, P, PAIRS, P)

    def by_half(v, width):
        return v.reshape(2, -1, width).transpose(0, 2, 1).reshape(2 * width, -1)

    def by_tile(v):
        return v[:MAIN].reshape(GROUPS, 2, TILES, P).transpose(3, 0, 1, 2), v[MAIN:].reshape(2, T_TILES, T_P).transpose(2, 0, 1)

    src_t, src_r = by_tile(src)
    dst_t, dst_r = by_tile(dst)
    e_main = np.zeros((GROUPS, 2, E_ROWS, HALF), e.dtype)
    e_main[:, :, :EDGE_F] = e[:MAIN].reshape(GROUPS, 2, HALF, EDGE_F).transpose(0, 1, 3, 2)
    e_ragged = np.zeros((2, E_ROWS, T_HALF), e.dtype)
    e_ragged[:, :EDGE_F] = e[MAIN:].reshape(2, T_HALF, EDGE_F).transpose(0, 2, 1)
    w_src = np.zeros((2, F, 2, F), w1.dtype)
    w_dst = np.zeros((2, F, 2, F), w1.dtype)
    w_edges = np.zeros((2, E_ROWS, 2, F), w1.dtype)
    for h in range(2):
        w_edges[h, :EDGE_F, h] = w1[:, 2 * F:].T
        w_src[h, :, h] = w1[:, :F].T
        w_dst[h, :, h] = w1[:, F:2 * F].T
    arrays = {
        "xt": xt, "x_nodes": by_half(x, F),
        "src_t": src_t.reshape(P, GROUPS, 2 * TILES), "src_r": src_r.reshape(T_P, 2 * T_TILES),
        "dst_t": dst_t.reshape(P, GROUPS, 2 * TILES), "dst_r": dst_r.reshape(T_P, 2 * T_TILES), "dst_h": dst[:MAIN].reshape(D_ROWS, D_HALVES, HALF),
        "dst_hr": dst[MAIN:].reshape(2, 1, T_HALF),
        "e_main": e_main.reshape(GROUPS, 2 * E_ROWS, HALF), "e_ragged": e_ragged.reshape(2 * E_ROWS, T_HALF),
        "x": x, "w_dst": w_dst.reshape(P, P), "w_src": w_src.reshape(P, P), "w_edges": w_edges.reshape(2 * E_ROWS, P), "b1": a["L0_gnn_b1"],
        "g1": a["L0_gnn_g1"], "bt1": a["L0_gnn_bt1"], "g2": a["L0_gnn_g2"], "bt2": a["L0_gnn_bt2"],
        "g3": a["L0_gnn_g3"], "bt3": a["L0_gnn_bt3"],
    }
    arrays = {k: np.ascontiguousarray(v) for k, v in arrays.items()}
    nc = bacc.Bacc("TRN2", target_bir_lowering=False, num_devices=1)
    args = [nc.dram_tensor(k, v.shape, mybir.dt.from_np(v.dtype), kind="ExternalInput").ap() for k, v in arrays.items()]
    out = nc.dram_tensor("out", (P, N_NODES // 2), F32, kind="ExternalOutput").ap()
    build(nc, *args, out)
    r = run_bass_kernel_spmd(nc, [arrays], core_ids=[0])
    return by_half(np.asarray(r.results[0]["out"]), N_NODES // 2).reshape(N_NODES, F)
```
